# Optimizing a Trainium2 kernel written in Bass

```python
import numpy as np
import jax
import jax.numpy as jnp

def _softmax(x, axis=-1):
    return jax.nn.softmax(x, axis=axis)

def _gelu(x):
    return jax.nn.gelu(x, approximate=True)

def _silu(x):
    return jax.nn.silu(x)

def _sigmoid(x):
    return jax.nn.sigmoid(x)

def _layernorm(x, axis=-1, eps=1e-05):
    m = jnp.mean(x, axis=axis, keepdims=True)
    v = jnp.var(x, axis=axis, keepdims=True)
    return (x - m) / jnp.sqrt(v + eps)

def _scatter_add(tgt, idx, src, axis=0):
    return tgt.at[idx].add(src)

def _segment_sum(src, seg, n):
    return jax.ops.segment_sum(src, seg, n)
kernel_name = 'mk_gnn_resnorm_d1_gnn_r8_ed59f7'

def setup_inputs(seed: int=0):
    np.random.seed(seed)
    _w = jnp.asarray

    def _rec_inputs():
        import jax
        import jax.numpy as jnp
        _gk = jax.random.key(seed)
        x = -0.0006008 + 1.001 * jax.random.normal(jax.random.fold_in(_gk, 1), (6250, 128), jnp.float32)
        src = jax.random.randint(jax.random.fold_in(_gk, 2), (200000,), 0, 6250, jnp.int32)
        dst = jnp.minimum((6250 * jax.random.uniform(jax.random.fold_in(_gk, 3), (200000,)) ** 2.0).astype(jnp.int32), 49999)
        _o = jnp.argsort(dst, stable=True)
        src = src[_o]
        dst = dst[_o]
        edge_attr_20 = jax.random.uniform(jax.random.fold_in(_gk, 12), (200000, 20), jnp.float32, 0.0, 1)
        edge_weight = jax.random.uniform(jax.random.fold_in(_gk, 13), (200000,), jnp.float32, 0.0, 0.999998)
        return (x, src, dst, edge_attr_20, edge_weight)
    x, src, dst, edge_attr_20, edge_weight = _rec_inputs()

    def _L0_gnn_setup():
        import jax, jax.numpy as jnp
        import numpy as np
        N_ATOMS = 2500
        N_EDGES = 80000
        N_BASIS = 128
        N_RBF = 20
        N_FILT = 128

        def ssp(v):
            return jax.nn.softplus(v) - jnp.log(2.0).astype(v.dtype)
        key = jax.random.key(seed)
        ks = jax.random.split(key, 16)
        s = lambda fan_in: 1.0 / np.sqrt(fan_in)
        return {'x': jax.random.normal(ks[0], (N_ATOMS, N_BASIS), dtype=jnp.float32), 'f_ij': jax.random.uniform(ks[1], (N_EDGES, N_RBF), dtype=jnp.float32), 'rcut_ij': jax.random.uniform(ks[2], (N_EDGES,), dtype=jnp.float32), 'idx_i': jax.random.randint(ks[3], (N_EDGES,), 0, N_ATOMS), 'idx_j': jax.random.randint(ks[4], (N_EDGES,), 0, N_ATOMS), 'W_in2f': jax.random.normal(ks[5], (N_BASIS, N_FILT), dtype=jnp.float32) * s(N_BASIS), 'W_filt1': jax.random.normal(ks[6], (N_RBF, N_FILT), dtype=jnp.float32) * s(N_RBF), 'b_filt1': jnp.zeros((N_FILT,), dtype=jnp.float32), 'W_filt2': jax.random.normal(ks[7], (N_FILT, N_FILT), dtype=jnp.float32) * s(N_FILT), 'b_filt2': jnp.zeros((N_FILT,), dtype=jnp.float32), 'W_out1': jax.random.normal(ks[8], (N_FILT, N_BASIS), dtype=jnp.float32) * s(N_FILT), 'b_out1': jnp.zeros((N_BASIS,), dtype=jnp.float32), 'W_out2': jax.random.normal(ks[9], (N_BASIS, N_BASIS), dtype=jnp.float32) * s(N_BASIS), 'b_out2': jnp.zeros((N_BASIS,), dtype=jnp.float32)}
    _L0_gnn_all = _L0_gnn_setup()
    _L0_gnn_in = {k: v for k, v in _L0_gnn_all.items() if k in ('W_in2f', 'W_filt1', 'b_filt1', 'W_filt2', 'b_filt2', 'W_out1', 'b_out1', 'W_out2', 'b_out2')}
    del _L0_gnn_all
    return {'x': x, 'src': src, 'dst': dst, 'edge_attr_20': edge_attr_20, 'edge_weight': edge_weight, 'L0_gnn_W_in2f': _L0_gnn_in['W_in2f'], 'L0_gnn_W_filt1': _L0_gnn_in['W_filt1'], 'L0_gnn_b_filt1': _L0_gnn_in['b_filt1'], 'L0_gnn_W_filt2': _L0_gnn_in['W_filt2'], 'L0_gnn_b_filt2': _L0_gnn_in['b_filt2'], 'L0_gnn_W_out1': _L0_gnn_in['W_out1'], 'L0_gnn_b_out1': _L0_gnn_in['b_out1'], 'L0_gnn_W_out2': _L0_gnn_in['W_out2'], 'L0_gnn_b_out2': _L0_gnn_in['b_out2']}

def reference(x, src, dst, edge_attr_20, edge_weight, L0_gnn_W_in2f, L0_gnn_W_filt1, L0_gnn_b_filt1, L0_gnn_W_filt2, L0_gnn_b_filt2, L0_gnn_W_out1, L0_gnn_b_out1, L0_gnn_W_out2, L0_gnn_b_out2):
    import jax
    import jax.numpy as jnp

    def _L0_gnn_ref(x, f_ij, rcut_ij, idx_i, idx_j, W_in2f, W_filt1, b_filt1, W_filt2, b_filt2, W_out1, b_out1, W_out2, b_out2):
        import jax, jax.numpy as jnp
        import numpy as np
        N_ATOMS = 2500
        N_EDGES = 80000
        N_BASIS = 128
        N_RBF = 20
        N_FILT = 128

        def ssp(v):
            return jax.nn.softplus(v) - jnp.log(2.0).astype(v.dtype)
        n_atoms = x.shape[0]
        h = x @ W_in2f
        Wij = ssp(f_ij @ W_filt1 + b_filt1) @ W_filt2 + b_filt2
        Wij = Wij * rcut_ij[:, None]
        x_ij = h[idx_j] * Wij
        agg = jax.ops.segment_sum(x_ij, idx_i, num_segments=n_atoms)
        out = ssp(agg @ W_out1 + b_out1) @ W_out2 + b_out2
        return out
    x = _layernorm(x + _L0_gnn_ref(x, edge_attr_20, edge_weight, src, dst, L0_gnn_W_in2f, L0_gnn_W_filt1, L0_gnn_b_filt1, L0_gnn_W_filt2, L0_gnn_b_filt2, L0_gnn_W_out1, L0_gnn_b_out1, L0_gnn_W_out2, L0_gnn_b_out2), axis=-1)
    return x

_drawn_inputs = setup_inputs


def setup_inputs(seed=0):
    import zlib

    import numpy as np

    out = dict(_drawn_inputs(seed))
    spreads = {'L0_gnn_b_filt1': (0.0, 0.1),
     'L0_gnn_b_filt2': (0.0, 0.1),
     'L0_gnn_b_out1': (0.0, 0.1),
     'L0_gnn_b_out2': (0.0, 0.1)}
    factors = {}
    for name, (base, spread) in spreads.items():
        noise = np.random.default_rng([zlib.crc32(name.encode()), seed]).standard_normal(out[name].shape)
        drawn = base * np.exp(spread * noise) if base else spread * noise
        out[name] = jnp.asarray(drawn.astype(out[name].dtype))
    for name, factor in factors.items():
        out[name] = (out[name] * factor).astype(out[name].dtype)
    return out
```

```python
import math
from contextlib import ExitStack

import concourse.bass as bass
import numpy as np
from concourse import mybir
from concourse.alu_op_type import AluOpType as ALU

P = 128
NODES, DIM, RBF = 6250, 128, 20
EDGES = 200000
TILES = 4
GROUP = TILES * P
GROUPS = -(-EDGES // GROUP)
GROUPS += GROUPS % 2
EDGES_PAD = GROUPS * GROUP
CHUNK = 4 * P
FULL_CHUNKS = NODES // CHUNK
NODE_ROWS = -(-NODES // P) * P
TABLE_ROWS = NODE_ROWS + P
WINDOW_ROWS = TABLE_ROWS
LAST_H = WINDOW_ROWS - FULL_CHUNKS * CHUNK
LAST_OUT = NODE_ROWS - FULL_CHUNKS * CHUNK
PAD_SRC = NODES
GROUP_PARTS = 98
PER_PART = GROUPS // GROUP_PARTS
COLS = 13
LN2 = math.log(2.0)
EXP_MAX = 2.0 ** 60
EPS = 1e-5
BIAS_ROWS = 96
FILL = 3
PAIRS = (GROUPS - 2 - FILL) // 2

assert GROUP_PARTS * PER_PART == GROUPS and LAST_OUT == P and LAST_H == 2 * P

F32, BF16 = mybir.dt.float32, mybir.dt.bfloat16
I32, U16 = mybir.dt.int32, mybir.dt.uint16
ACT = mybir.ActivationFunctionType
AX_X = mybir.AxisListType.X



def number(g):
    return 2 * g[0] + g[1]


def after(g):
    return 2 * g[0] + (g[1] + 1)


def landed(g):
    return 16 * g[0] + 16 * (g[1] // 2 + 1)


def scattered(g):
    return 32 * g[0] + 16 * (g[1] + 1)


def plus(g, n):
    return g[0], g[1] + n


def exists(g):
    return not isinstance(g[0], int) or 0 <= g[1] < GROUPS


def build(nc, t):
    with ExitStack() as ctx:
        def sb(name, shape, dt):
            return ctx.enter_context(nc.sbuf_tensor(name, shape, dt))

        def sem(name):
            return ctx.enter_context(nc.semaphore(name))

        def dram(name, shape, dt):
            return nc.dram_tensor(name, shape, dt, kind="Internal").ap()

        dst16 = dram("dst16", (EDGES_PAD,), U16)
        src16 = dram("src16", (EDGES_PAD,), U16)
        base_d = dram("window_base", (GROUPS,), F32)
        spread_d = dram("window_spread", (GROUPS,), F32)
        h_parts = dram("h_parts", (WINDOW_ROWS, 3 * DIM), BF16)
        tables = [dram(f"table{k}", (TABLE_ROWS, DIM), F32) for k in range(TILES)]

        ident = sb("ident", [P, P], F32)
        earlier = sb("earlier", [P, P], F32)
        row_id = sb("row_id", [P, 1], F32)
        spare_row = sb("spare_row", [P, 1], F32)
        minus_ln2 = sb("minus_ln2", [P, P], F32)
        ones_bias = sb("ones_bias", [BIAS_ROWS, P], BF16)
        w_in = sb("w_in", [P, DIM], F32)
        w_f1 = sb("w_f1", [RBF, DIM], F32)
        w_f2 = sb("w_f2", [P, DIM], F32)
        w_o1 = sb("w_o1", [P, DIM], F32)
        w_o2 = sb("w_o2", [P, DIM], F32)
        b_f1 = sb("b_f1", [P, 1], F32)
        b_o1 = sb("b_o1", [P, 1], F32)
        b_f2 = sb("b_f2", [P, DIM], F32)
        b_o2 = sb("b_o2", [P, DIM], F32)
        bias_tmp = sb("bias_tmp", [P, 2, 4, DIM], F32)
        bias_hi = sb("bias_hi", [P, 2, 3, DIM], BF16)
        bias_f = sb("bias_f", [BIAS_ROWS, TILES, DIM], BF16)
        bias_o = sb("bias_o", [BIAS_ROWS, TILES, DIM], BF16)

        edge_cols = sb("edge_cols", [P, GROUPS, COLS], F32)
        src_i = sb("src_i", [P, GROUPS * TILES], I32)
        weight_c = sb("weight_c", [P, GROUPS * TILES], F32)
        dst_g = sb("dst_g", [GROUP_PARTS, PER_PART, GROUP], I32)
        src_g = sb("src_g", [GROUP_PARTS, PER_PART, GROUP], I32)
        dst_g16 = sb("dst_g16", [GROUP_PARTS, PER_PART * GROUP], U16)
        src_g16 = sb("src_g16", [GROUP_PARTS, PER_PART * GROUP], U16)
        dst_low = sb("dst_low", [GROUP_PARTS, PER_PART], F32)
        dst_high = sb("dst_high", [GROUP_PARTS, PER_PART], F32)
        dst_spread = sb("dst_spread", [GROUP_PARTS, PER_PART], F32)
        base_all = sb("base_all", [P, GROUPS], F32)
        base_i = sb("base_i", [1, GROUPS], I32)
        spread_row = sb("spread_row", [1, GROUPS], F32)
        widest = sb("widest", [1, 1], F32)
        narrow = sb("narrow", [1, 1], I32)

        x_t = sb("x_t", [P, 2, CHUNK], F32)
        h_out = sb("h_out", [P, 2, 4, 3, DIM], BF16)
        h_rest = sb("h_rest", [P, 2, 4, DIM], F32)
        rows = sb("rows", [P, TABLE_ROWS // P * DIM], F32)

        f_t = sb("f_t", [RBF, 2, GROUP], F32)
        dst_b = sb("dst_b", [P, 2, GROUP], U16)
        src_b = sb("src_b", [P, 2, GROUP], U16)
        window = sb("window", [P, 2, 3, DIM], BF16)
        cols = sb("cols", [P, 2, COLS], F32)
        soft = sb("soft", [P, 2, GROUP], F32)
        hidden = sb("hidden", [P, 2, GROUP], F32)
        pick = sb("pick", [P, 2, GROUP], BF16)
        h_dst = sb("h_dst", [P, 2, GROUP], F32)
        same = sb("same", [P, 2, GROUP], F32)
        n_same = sb("n_same", [P, 2, TILES], F32)
        moved = sb("moved", [P, 2, TILES], F32)
        row_of = sb("row_of", [P, 2, TILES], F32)
        index = sb("index", [P, 2, TILES], I32)
        message = sb("message", [P, 2, GROUP], F32)
        total = sb("total", [P, 2, GROUP], F32)
        dst_i = sb("dst_i", [P, 2, TILES], I32)
        h_rows = sb("h_rows", [P, 2, TILES, 3, DIM], BF16)

        parts = sb("parts", [P, 2, TILES, CHUNK], F32)
        half_sum = sb("half_sum", [P, 2, 2, CHUNK], F32)
        agg_t = sb("agg_t", [P, 2, CHUNK], F32)
        x_rows = sb("x_rows", [P, 2, CHUNK], F32)
        y_rows = sb("y_rows", [P, 2, CHUNK], F32)
        stats = sb("stats", [P, 2, 4, 6], F32)
        chunk_mean_var = sb("chunk_mean_var", [P, 2, 4, 2], F32)
        mean_var = sb("mean_var", [P, NODE_ROWS // P, 2], F32)
        deviation = sb("deviation", [P, NODE_ROWS // P], F32)
        inv_dev = sb("inv_dev", [P, NODE_ROWS // P], F32)
        eps_col = sb("eps_col", [P, 1], F32)

        pre_psum = ctx.enter_context(nc.psum_tensor("pre_psum", [P, 2, GROUP], F32))
        filter_psum = ctx.enter_context(nc.psum_tensor("filter_psum", [P, 2, GROUP], F32))
        gather_psum = ctx.enter_context(nc.psum_tensor("gather_psum", [P, 2, GROUP], F32))
        total_psum = ctx.enter_context(nc.psum_tensor("total_psum", [P, 2, GROUP], F32))

        dst_loaded, src_loaded = sem("dst_loaded"), sem("src_loaded")
        cols_loaded, consts_loaded = sem("cols_loaded"), sem("consts_loaded")
        zeros_made, tables_zeroed = sem("zeros_made"), sem("tables_zeroed")
        const_step, consts_made = sem("const_step"), sem("consts_made")
        dst16_made, src16_made, edges16_stored = sem("dst16_made"), sem("src16_made"), sem("edges16_stored")
        spans_made, spans_stored, spans_loaded = sem("spans_made"), sem("spans_stored"), sem("spans_loaded")
        dve_step = sem("dve_step")
        cols_made, flag_made = sem("cols_made"), sem("flag_made")
        bias_mm, bias_parts, bias_made = sem("bias_mm"), sem("bias_parts"), sem("bias_made")
        x_t_loaded = [sem(f"x_t_loaded{b}") for b in range(2)]
        h_mm, h_hi, h_left, h_mid, h_lo = (sem(n) for n in ("h_mm", "h_hi", "h_left", "h_mid", "h_lo"))
        h_stored = [sem(f"h_stored{b}") for b in range(2)]

        f_loaded = [sem(f"f_loaded{b}") for b in range(2)]
        dst_b_loaded = [sem(f"dst_b_loaded{b}") for b in range(2)]
        src_b_loaded = [sem(f"src_b_loaded{b}") for b in range(2)]
        window_loaded = [sem(f"window_loaded{b}") for b in range(2)]
        pre_done, exp_done, clamp_done = sem("pre_done"), sem("exp_done"), sem("clamp_done")
        ln_done, hidden_done, filter_done = sem("ln_done"), sem("hidden_done"), sem("filter_done")
        cols_done, pick_done = sem("cols_done"), sem("pick_done")
        gather_done, h_dst_done = sem("gather_done"), sem("h_dst_done")
        same_done, moved_done = sem("same_done"), sem("moved_done")
        row_done, index_done = sem("row_done"), sem("index_done")
        message_done, total_mm_done, total_done = sem("message_done"), sem("total_mm_done"), sem("total_done")
        table_added = [sem(f"table_added{k}") for k in range(TILES)]
        rows_gathered = [sem(f"rows_gathered{b}") for b in range(2)]
        h_sum_step, pool_turns = sem("h_sum_step"), sem("pool_turns")

        parts_loaded = [sem(f"parts_loaded{b}") for b in range(2)]
        e_half_a, e_half_b, e_agg_t, e_agg_sb, e_pre = sem("e_half_a"), sem("e_half_b"), sem("e_agg_t"), sem("e_agg_sb"), sem("e_pre")
        e_exp, e_clamp, e_ln, e_hidden = sem("e_exp"), sem("e_clamp"), sem("e_ln"), sem("e_hidden")
        e_out, e_row, e_stats, e_aggr = sem("e_out"), sem("e_row"), sem("e_stats"), sem("e_aggr")
        e_moments, e_kept = sem("e_moments"), sem("e_kept")
        e_dev, e_inv, e_norm = sem("e_dev"), sem("e_inv"), sem("e_norm")
        out_stored = sem("out_stored")

        block = ctx.enter_context(nc.Block())

        def run_groups(eng, step, first=-1):
            for i in range(first, FILL):
                step((0, i))
            with eng.Fori(0, PAIRS) as j:
                step((j, FILL))
                step((j, FILL + 1))
            for i in range(FILL + 2 * PAIRS, GROUPS + 1):
                step((0, i))

        def run_chunks(eng, step, last):
            step((0, 0), CHUNK // P)
            step((0, 1), CHUNK // P)
            with eng.Fori(0, FULL_CHUNKS // 2 - 1) as j:
                step((j, 2), CHUNK // P)
                step((j, 3), CHUNK // P)
            step((0, FULL_CHUNKS), last // P)

        def previous(eng, s, g, count, n=2):
            if not isinstance(g[0], int) or g[1] >= n:
                eng.wait_ge(s, count(plus(g, -n)))

        def held(eng, count, g):
            if isinstance(g[0], int):
                return count(g) if g[1] >= 0 else None
            return eng.snap(count(g))

        @block.sync
        def _(sp):
            sp.dma_start(dst_g[:, :, :], t["dst"].rearrange("(p g e) -> p g e", p=GROUP_PARTS, e=GROUP)
                         ).then_inc(dst_loaded, 16)
            sp.dma_start(src_g[:, :, :], t["src"].rearrange("(p g e) -> p g e", p=GROUP_PARTS, e=GROUP)
                         ).then_inc(src_loaded, 16)
            sp.dma_start(src_i[:, :], t["src_cols"]).then_inc(cols_loaded, 16)
            sp.dma_start(weight_c[:, :], t["weight_cols"]).then_inc(cols_loaded, 16)

            sp.wait_ge(spans_made, 2)
            sp.dma_start(base_d.rearrange("(p g) -> p g", p=GROUP_PARTS), dst_low[:, :]).then_inc(spans_stored, 16)
            sp.dma_start(spread_d.rearrange("(p g) -> p g", p=GROUP_PARTS), dst_spread[:, :]
                         ).then_inc(spans_stored, 16)
            sp.wait_ge(dst16_made, 1)
            sp.dma_start(dst16.rearrange("(p e) -> p e", p=GROUP_PARTS), dst_g16[:, :]).then_inc(edges16_stored, 16)
            sp.wait_ge(src16_made, 1)
            sp.dma_start(src16.rearrange("(p e) -> p e", p=GROUP_PARTS), src_g16[:, :]).then_inc(edges16_stored, 16)
            sp.wait_ge(spans_stored, 32)
            sp.dma_start(base_all[:, :], base_d.partition_broadcast(P)).then_inc(spans_loaded, 16)
            sp.dma_start(spread_row[:, :], spread_d.partition_broadcast(1)).then_inc(spans_loaded, 16)

            def load_x_t(c, tiles):
                b, n = c[1] % 2, number(c)
                previous(sp, h_mm, c, after)
                sp.dma_start(x_t[:, b, 0:tiles * P], t["x_t"][:, bass.ds(n * CHUNK, tiles * P)]
                             ).then_inc(x_t_loaded[b], 16)

            def store_h(c, tiles):
                b, n = c[1] % 2, number(c)
                sp.wait_ge(h_lo, after(c))
                sp.dma_start(h_parts[bass.ds(n * CHUNK, tiles * P), :].rearrange("(p t) d -> p t d", t=tiles),
                             h_out[:, b, 0:tiles, :, :].rearrange("p t k d -> p t (k d)")
                             ).then_inc(h_stored[b], 16)

            load_x_t((0, 0), CHUNK // P)
            load_x_t((0, 1), CHUNK // P)
            with sp.Fori(0, FULL_CHUNKS // 2 - 1) as j:
                for b in range(2):
                    store_h((j, b), CHUNK // P)
                    load_x_t((j, b + 2), CHUNK // P)
            store_h((0, FULL_CHUNKS - 2), CHUNK // P)
            load_x_t((0, FULL_CHUNKS), LAST_H // P)
            store_h((0, FULL_CHUNKS - 1), CHUNK // P)
            store_h((0, FULL_CHUNKS), LAST_H // P)
            for b in range(2):
                sp.wait_ge(h_stored[b], 16 * (FULL_CHUNKS // 2 + (b == 0)))
            sp.wait_ge(edges16_stored, 32)
            sp.wait_ge(flag_made, 1)
            is_narrow = sp.value_load(narrow[0:1, 0:1], min_val=0, max_val=1)

            def load_features(g):
                b = g[1] % 2
                before = held(sp, after, plus(g, -2))
                sp.wait_ge(flag_made, 1)
                if before is not None:
                    sp.wait_ge(pre_done, before)
                sp.dma_start(f_t[:, b, :], t["f_t"][:, bass.ds(number(g) * GROUP, GROUP)]).then_inc(f_loaded[b], 16)

            def load_src(g):
                b = g[1] % 2
                before = held(sp, after, plus(g, -2))
                sp.wait_ge(flag_made, 1)
                if before is not None:
                    sp.wait_ge(same_done, before)
                sp.dma_start(src_b[:, b, :], src16[bass.ds(number(g) * GROUP, GROUP)].partition_broadcast(P)
                             ).then_inc(src_b_loaded[b], 16)

            def step_narrow(i):
                if exists(plus(i, 3)):
                    load_features(plus(i, 3))
                g = plus(i, 2)
                b = g[1] % 2
                if exists(g):
                    before = held(sp, after, plus(g, -2))
                    sp.wait_ge(flag_made, 1)
                    if before is not None:
                        sp.wait_ge(pick_done, before)
                    sp.dma_start(dst_b[:, b, :], dst16[bass.ds(number(g) * GROUP, GROUP)].partition_broadcast(P)
                                 ).then_inc(dst_b_loaded[b], 16)
                    start = sp.value_load(base_i[0:1, bass.ds(number(g), 1)], min_val=0, max_val=NODES - 1)
                    previous(sp, gather_done, g, after)
                    sp.dma_start(window[:, b, :, :], h_parts[bass.ds(start, P), :].rearrange("n (k d) -> n k d", k=3)
                                 ).then_inc(window_loaded[b], 16)
                if exists(plus(i, 1)):
                    load_src(plus(i, 1))

            def step_general(i):
                if exists(plus(i, 3)):
                    load_features(plus(i, 3))
                g = plus(i, 2)
                b = g[1] % 2
                if exists(g):
                    if not isinstance(g[0], int) or g[1] >= 2:
                        sp.wait_ge(rows_gathered[b], 64 * g[0] + 64 * (g[1] // 2))
                    sp.dma_start(dst_i[:, b, :], t["dst_cols"][:, bass.ds(number(g) * TILES, TILES)]
                                 ).then_inc(dst_b_loaded[b], 16)
                if exists(plus(i, 1)):
                    load_src(plus(i, 1))

            with sp.If(is_narrow):
                run_groups(sp, step_narrow, -3)
            with sp.Else():
                run_groups(sp, step_general, -3)

            for k in range(TILES):
                sp.wait_ge(table_added[k], 16 * GROUPS)

            def load_chunk(c, tiles):
                b, n = c[1] % 2, number(c)
                previous(sp, e_row, c, after)
                span = bass.ds(n * CHUNK, tiles * P)
                for k in range(TILES):
                    sp.dma_start(parts[:, b, k, 0:tiles * DIM].rearrange("p (t d) -> p t d", d=DIM),
                                 tables[k][span, :].rearrange("(p t) d -> p t d", t=tiles)
                                 ).then_inc(parts_loaded[b], 16)
                sp.dma_start(x_rows[:, b, 0:tiles * DIM].rearrange("p (t d) -> p t d", d=DIM),
                             t["x"][span, :].rearrange("(p t) d -> p t d", t=tiles)).then_inc(parts_loaded[b], 16)

            run_chunks(sp, load_chunk, LAST_OUT)

            sp.wait_ge(e_norm, NODE_ROWS // P)
            full = FULL_CHUNKS * CHUNK
            sp.dma_start(t["out"][0:full, :].rearrange("(c p t) d -> p c t d", p=P, t=4),
                         rows[:, 0:FULL_CHUNKS * 4 * DIM].rearrange("p (c t d) -> p c t d", t=4, d=DIM)
                         ).then_inc(out_stored, 16)
            sp.dma_start(t["out"][full:NODES, :], rows[0:NODES - full, FULL_CHUNKS * 4 * DIM:NODE_ROWS // P * DIM]
                         ).then_inc(out_stored, 16)
            sp.wait_ge(out_stored, 32)

        @block.gpsimd
        def _(pool):
            pool.memset(earlier[:, :], 1.0).then_inc(const_step, 1)
            pool.memset(ident[:, :], 0.0).then_inc(const_step, 1)
            pool.memset(ones_bias[:, :], 1.0).then_inc(consts_made, 1)
            pool.memset(minus_ln2[:, :], -LN2).then_inc(consts_made, 1)
            pool.memset(eps_col[:, :], EPS).then_inc(consts_made, 1)
            pool.iota(row_id[:, :], pattern=[[0, 1]], base=0, channel_multiplier=1,
                      allow_small_or_imprecise_dtypes=True).then_inc(consts_made, 1)
            pool.iota(spare_row[:, :], pattern=[[0, 1]], base=NODE_ROWS, channel_multiplier=1,
                      allow_small_or_imprecise_dtypes=True).then_inc(consts_made, 1)
            pool.wait_ge(const_step, 2)
            pool.affine_select(out=earlier[:, :], in_=earlier[:, :], compare_op=ALU.is_ge, fill=0.0, base=0,
                               pattern=[[-1, P]], channel_multiplier=1).then_inc(consts_made, 1)
            pool.affine_select(out=ident[:, :], in_=ident[:, :], compare_op=ALU.not_equal, fill=1.0, base=0,
                               pattern=[[-1, P]], channel_multiplier=1).then_inc(consts_made, 1)

            pool.wait_ge(flag_made, 1)
            is_narrow = pool.value_load(narrow[0:1, 0:1], min_val=0, max_val=1)

            def scatter(g):
                b = g[1] % 2
                before = held(pool, scattered, plus(g, -1))
                pool.wait_ge(index_done, after(g))
                pool.wait_ge(total_done, after(g))
                if before is not None:
                    pool.wait_ge(table_added[0], before)
                pool.sem_inc(pool_turns, 1)
                for k in range(TILES):
                    pool.wait_ge(tables_zeroed, 16 * TILES)
                    if before is not None and k:
                        pool.wait_ge(table_added[k], before)
                    pool.indirect_dma_start(tables[k], bass.IndirectOffsetOnAxis(index[:, b, k:k + 1], 0),
                                            total[:, b, k * DIM:(k + 1) * DIM], None, compute_op=ALU.add
                                            ).then_inc(table_added[k], 16)

            def gather(g):
                b = g[1] % 2
                arrived = held(pool, landed, g)
                before = held(pool, after, plus(g, -2))
                pool.wait_ge(dst_b_loaded[b], arrived)
                if before is not None:
                    pool.wait_ge(h_dst_done, before)
                pool.sem_inc(pool_turns, 1)
                for k in range(TILES):
                    pool.indirect_dma_start(h_rows[:, b, k, :, :].rearrange("p k d -> p (k d)"), None, h_parts,
                                            bass.IndirectOffsetOnAxis(dst_i[:, b, k:k + 1], 0)
                                            ).then_inc(rows_gathered[b], 16)

            def step_narrow(i):
                if exists(plus(i, -1)):
                    scatter(plus(i, -1))

            def step_general(i):
                if exists(plus(i, 1)):
                    gather(plus(i, 1))
                if exists(plus(i, -1)):
                    scatter(plus(i, -1))

            pool.wait_ge(tables_zeroed, 16 * TILES)
            with pool.If(is_narrow):
                run_groups(pool, step_narrow)
            with pool.Else():
                for b in range(2):
                    pool.wait_ge(h_stored[b], 16 * (FULL_CHUNKS // 2 + (b == 0)))
                run_groups(pool, step_general)

            def half(c, tiles):
                b = c[1] % 2
                pool.wait_ge(parts_loaded[b], 80 * c[0] + 80 * (c[1] // 2 + 1))
                previous(pool, e_agg_t, c, after)
                pool.tensor_tensor(half_sum[:, b, 0, 0:tiles * DIM], parts[:, b, 0, 0:tiles * DIM],
                                   parts[:, b, 1, 0:tiles * DIM], ALU.add).then_inc(e_half_a, 1)

            run_chunks(pool, half, LAST_OUT)

        @block.scalar
        def _(act):
            act.dma_start(w_in[:, :], t["w_in"]).then_inc(consts_loaded, 16)
            act.dma_start(w_f1[:, :], t["w_f1"]).then_inc(consts_loaded, 16)
            act.dma_start(w_f2[:, :], t["w_f2"]).then_inc(consts_loaded, 16)
            act.dma_start(w_o1[:, :], t["w_o1"]).then_inc(consts_loaded, 16)
            act.dma_start(w_o2[:, :], t["w_o2"]).then_inc(consts_loaded, 16)
            act.dma_start(b_f1[:, :], t["b_f1"].rearrange("(p a) -> p a", a=1)).then_inc(consts_loaded, 16)
            act.dma_start(b_o1[:, :], t["b_o1"].rearrange("(p a) -> p a", a=1)).then_inc(consts_loaded, 16)
            act.dma_start(b_f2[:, :], t["b_f2"].partition_broadcast(P)).then_inc(consts_loaded, 16)
            act.dma_start(b_o2[:, :], t["b_o2"].partition_broadcast(P)).then_inc(consts_loaded, 16)
            act.wait_ge(zeros_made, 1)
            for k in range(TILES):
                act.dma_start(tables[k].rearrange("(p r) d -> p (r d)", p=P), rows[:, :]).then_inc(tables_zeroed, 16)

            act.preload_act_table_set("natural_log_exp_and_others")

            def split_h(c, tiles):
                b = c[1] % 2
                act.wait_ge(h_mm, after(c))
                previous(act, h_stored[b], c, landed)
                act.activation(h_out[:, b, 0:tiles, 0, :],
                               pre_psum[:, b, 0:tiles * DIM].rearrange("p (t d) -> p t d", d=DIM), ACT.Copy
                               ).then_inc(h_hi, 1)
                act.wait_ge(h_left, after(c))
                act.activation(h_out[:, b, 0:tiles, 1, :], h_rest[:, b, 0:tiles, :], ACT.Copy).then_inc(h_mid, 1)

            run_chunks(act, split_h, LAST_H)
            act.wait_ge(consts_loaded, 16 * 9)
            act.wait_ge(consts_made, 7)
            act.wait_ge(flag_made, 1)
            is_narrow = act.value_load(narrow[0:1, 0:1], min_val=0, max_val=1)
            act.wait_ge(cols_made, 4)

            def exponential(g):
                b = g[1] % 2
                act.wait_ge(pre_done, after(g))
                previous(act, hidden_done, g, after)
                act.activation(soft[:, b, :], pre_psum[:, b, :], ACT.Exp, bias=b_f1[:, 0:1]).then_inc(exp_done, 1)

            def columns(g):
                b = g[1] % 2
                previous(act, message_done, g, after)
                act.activation(cols[:, b, :], edge_cols[:, bass.ds(number(g), 1), :].rearrange("p a c -> p (a c)"),
                               ACT.Copy).then_inc(cols_done, 1)

            def logarithm(g):
                b = g[1] % 2
                act.wait_ge(clamp_done, after(g))
                act.activation(soft[:, b, :], soft[:, b, :], ACT.Ln, bias=1.0).then_inc(ln_done, 1)

            def copy_total(g):
                b = g[1] % 2
                act.wait_ge(total_mm_done, after(g))
                for k in range(TILES):
                    previous(act, table_added[k], g, scattered)
                act.activation(total[:, b, :], total_psum[:, b, :], ACT.Copy).then_inc(total_done, 1)

            def copy_h_dst(g):
                b = g[1] % 2
                act.wait_ge(gather_done, after(g))
                previous(act, message_done, g, after)
                act.activation(h_dst[:, b, :], gather_psum[:, b, :], ACT.Copy).then_inc(h_dst_done, 1)

            def step(i, narrow_form):
                if exists(plus(i, 1)):
                    exponential(plus(i, 1))
                    columns(plus(i, 1))
                    logarithm(plus(i, 1))
                if exists(plus(i, -1)):
                    copy_total(plus(i, -1))
                if narrow_form and exists(plus(i, 1)):
                    copy_h_dst(plus(i, 1))

            with act.If(is_narrow):
                run_groups(act, lambda i: step(i, True))
            with act.Else():
                run_groups(act, lambda i: step(i, False))

            def chunk(c, tiles):
                b, n = c[1] % 2, tiles * P
                act.wait_ge(e_agg_t, after(c))
                previous(act, e_pre, c, after)
                act.activation(agg_t[:, b, 0:n], filter_psum[:, b, 0:n], ACT.Copy).then_inc(e_agg_sb, 1)
                act.wait_ge(e_pre, after(c))
                previous(act, e_hidden, c, after)
                act.activation(soft[:, b, 0:n], pre_psum[:, b, 0:n], ACT.Exp, bias=b_o1[:, 0:1]).then_inc(e_exp, 1)
                act.wait_ge(e_clamp, after(c))
                act.activation(soft[:, b, 0:n], soft[:, b, 0:n], ACT.Ln, bias=1.0).then_inc(e_ln, 1)
                act.wait_ge(e_row, after(c))
                act.activation(rows[:, bass.ds(number(c) * CHUNK, n)], y_rows[:, b, 0:n], ACT.Copy).then_inc(e_kept, 1)

            run_chunks(act, chunk, LAST_OUT)
            act.wait_ge(e_moments, FULL_CHUNKS + 1)
            act.activation(deviation[:, :], mean_var[:, :, 1], ACT.Sqrt, bias=eps_col[:, 0:1]).then_inc(e_dev, 1)

        @block.vector
        def _(dve):
            dve.wait_ge(dst_loaded, 16)
            dve.tensor_reduce(dst_low[:, :], dst_g[:, :, :], AX_X, ALU.min).then_inc(spans_made, 1)
            dve.tensor_reduce(dst_high[:, :], dst_g[:, :, :], AX_X, ALU.max).then_inc(dve_step, 1)
            dve.wait_ge(spans_made, 1)
            dve.wait_ge(dve_step, 1)
            dve.tensor_tensor(dst_spread[:, :], dst_high[:, :], dst_low[:, :], ALU.subtract).then_inc(spans_made, 1)
            dve.tensor_copy(dst_g16[:, :], dst_g[:, :, :].rearrange("p g e -> p (g e)")).then_inc(dst16_made, 1)
            dve.wait_ge(src_loaded, 16)
            dve.tensor_copy(src_g16[:, :], src_g[:, :, :].rearrange("p g e -> p (g e)")).then_inc(src16_made, 1)
            dve.memset(rows[:, :], 0.0).then_inc(zeros_made, 1)

            def per_tile(a, b):
                return edge_cols[:, :, a:b]

            def grouped(x):
                return x.rearrange("p (g k) -> p g k", k=TILES)

            dve.wait_ge(cols_loaded, 32)
            dve.wait_ge(consts_made, 7)
            dve.tensor_copy(per_tile(0, 4), grouped(src_i[:, :])).then_inc(cols_made, 1)
            dve.tensor_copy(per_tile(4, 8), grouped(weight_c[:, :])).then_inc(cols_made, 1)
            dve.tensor_scalar(per_tile(8, 12), grouped(src_i[:, :]), -1.0, spare_row[:, 0:1], ALU.mult, ALU.add
                              ).then_inc(cols_made, 1)

            dve.wait_ge(consts_loaded, 16 * 9)
            dve.wait_ge(bias_mm, 1)
            dve.tensor_tensor(bias_tmp[:, 0, 0, :], total_psum[:, 0, 0:DIM], b_f2[:, :], ALU.add).then_inc(dve_step, 1)
            dve.tensor_tensor(bias_tmp[:, 1, 0, :], total_psum[:, 0, DIM:2 * DIM], b_o2[:, :], ALU.add
                              ).then_inc(dve_step, 1)
            steps = 3
            for part in range(3):
                dve.wait_ge(dve_step, steps)
                dve.tensor_copy(bias_hi[:, :, part, :], bias_tmp[:, :, part, :]).then_inc(dve_step, 1)
                steps += 1
                if part < 2:
                    dve.wait_ge(dve_step, steps)
                    dve.tensor_tensor(bias_tmp[:, :, part + 1, :], bias_tmp[:, :, part, :], bias_hi[:, :, part, :],
                                      ALU.subtract).then_inc(dve_step, 1)
                    steps += 1
            dve.memset(bias_f[:, :, :], 0.0).then_inc(dve_step, 1)
            dve.memset(bias_o[:, :, :], 0.0).then_inc(dve_step, 1)
            dve.wait_ge(dve_step, steps + 2)
            for which, dest in enumerate((bias_f, bias_o)):
                for part in range(3):
                    q = 32 * part
                    dve.tensor_copy(dest[q:q + 1, :, :], bias_hi[q:q + 1, which:which + 1, part, :]
                                    .to_broadcast([1, TILES, DIM])).then_inc(bias_made, 1)

            def split_h(c, tiles):
                b = c[1] % 2
                dve.wait_ge(h_hi, after(c))
                previous(dve, h_mid, c, after)
                dve.tensor_tensor(h_rest[:, b, 0:tiles, :],
                                  pre_psum[:, b, 0:tiles * DIM].rearrange("p (t d) -> p t d", d=DIM),
                                  h_out[:, b, 0:tiles, 0, :], ALU.subtract).then_inc(h_left, 1)
                dve.wait_ge(h_mid, after(c))
                dve.wait_ge(h_left, after(c))
                dve.tensor_tensor(h_out[:, b, 0:tiles, 2, :], h_rest[:, b, 0:tiles, :], h_out[:, b, 0:tiles, 1, :],
                                  ALU.subtract).then_inc(h_lo, 1)

            dve.wait_ge(spans_loaded, 32)
            dve.tensor_scalar(edge_cols[:, :, 12], base_all[:, :], row_id[:, 0:1], None, ALU.add).then_inc(cols_made, 1)
            dve.tensor_copy(base_i[:, :], base_all[0:1, :]).then_inc(dve_step, 1)
            dve.tensor_reduce(widest[:, :], spread_row[:, :], AX_X, ALU.max).then_inc(dve_step, 1)
            dve.wait_ge(dve_step, steps + 4)
            dve.tensor_scalar(narrow[:, :], widest[:, :], float(P) - 0.5, None, ALU.is_lt).then_inc(flag_made, 1)
            run_chunks(dve, split_h, LAST_H)
            dve.wait_ge(flag_made, 1)
            is_narrow = dve.value_load(narrow[0:1, 0:1], min_val=0, max_val=1)
            dve.wait_ge(cols_made, 4)

            def compare_src(g):
                b = g[1] % 2
                dve.wait_ge(cols_done, after(g))
                dve.wait_ge(src_b_loaded[b], landed(g))
                previous(dve, total_mm_done, g, after)
                for k in range(TILES):
                    tile = slice(k * P, (k + 1) * P)
                    last = dve.scalar_tensor_tensor(same[:, b, tile], src_b[:, b, tile], cols[:, b, k:k + 1],
                                                    earlier[:, :], ALU.is_equal, ALU.mult,
                                                    accum_out=n_same[:, b, k:k + 1])
                last.then_inc(same_done, 1)

            def compare_dst(g):
                b = g[1] % 2
                dve.wait_ge(cols_done, after(g))
                dve.wait_ge(dst_b_loaded[b], landed(g))
                previous(dve, gather_done, g, after)
                dve.tensor_scalar(pick[:, b, :], dst_b[:, b, :], cols[:, b, 12:13], None, ALU.is_equal
                                  ).then_inc(pick_done, 1)

            def move_repeated(g):
                b = g[1] % 2
                dve.wait_ge(same_done, after(g))
                dve.scalar_tensor_tensor(moved[:, b, :], n_same[:, b, :], 1.5, cols[:, b, 8:12],
                                         ALU.is_gt, ALU.mult).then_inc(moved_done, 1)

            def add_src(g):
                b = g[1] % 2
                dve.wait_ge(moved_done, after(g))
                dve.tensor_tensor(row_of[:, b, :], moved[:, b, :], cols[:, b, 0:4], ALU.add).then_inc(row_done, 1)

            def make_index(g):
                b = g[1] % 2
                dve.wait_ge(row_done, after(g))
                for k in range(TILES):
                    previous(dve, table_added[k], g, scattered)
                dve.tensor_copy(index[:, b, :], row_of[:, b, :]).then_inc(index_done, 1)

            def clamp(g):
                b = g[1] % 2
                dve.wait_ge(exp_done, after(g))
                dve.tensor_scalar(soft[:, b, :], soft[:, b, :], EXP_MAX, None, ALU.min).then_inc(clamp_done, 1)

            def finish_hidden(g):
                b = g[1] % 2
                dve.wait_ge(ln_done, after(g))
                previous(dve, filter_done, g, after)
                dve.scalar_tensor_tensor(hidden[:, b, :], pre_psum[:, b, :], b_f1[:, 0:1], soft[:, b, :],
                                         ALU.add, ALU.max).then_inc(hidden_done, 1)

            def sum_parts(g):
                b = g[1] % 2
                dve.wait_ge(rows_gathered[b], 64 * g[0] + 64 * (g[1] // 2 + 1))
                h3 = h_dst[:, b, :].rearrange("p (k d) -> p k d", d=DIM)
                dve.tensor_tensor(h3, h_rows[:, b, :, 0, :], h_rows[:, b, :, 1, :], ALU.add).then_inc(h_sum_step, 1)
                dve.wait_ge(h_sum_step, after(g))
                dve.tensor_tensor(h3, h3, h_rows[:, b, :, 2, :], ALU.add).then_inc(h_dst_done, 1)

            def multiply(g):
                b = g[1] % 2
                dve.wait_ge(filter_done, after(g))
                dve.wait_ge(h_dst_done, after(g))
                previous(dve, total_mm_done, g, after)
                for k in range(TILES):
                    d = slice(k * DIM, (k + 1) * DIM)
                    last = dve.scalar_tensor_tensor(message[:, b, d], filter_psum[:, b, d], cols[:, b, 4 + k:5 + k],
                                                    h_dst[:, b, d], ALU.mult, ALU.mult)
                last.then_inc(message_done, 1)

            def step(i, narrow_form):
                if exists(i):
                    compare_src(i)
                if exists(plus(i, 1)) and narrow_form:
                    compare_dst(plus(i, 1))
                if exists(plus(i, 1)):
                    clamp(plus(i, 1))
                if exists(plus(i, -1)):
                    make_index(plus(i, -1))
                if exists(i):
                    move_repeated(i)
                    add_src(i)
                if exists(plus(i, 1)):
                    finish_hidden(plus(i, 1))
                if exists(i):
                    if not narrow_form:
                        sum_parts(i)
                    multiply(i)

            with dve.If(is_narrow):
                run_groups(dve, lambda i: step(i, True))
            with dve.Else():
                run_groups(dve, lambda i: step(i, False))

            def chunk(c, tiles):
                b, n, first = c[1] % 2, tiles * P, number(c) * 4
                dve.wait_ge(parts_loaded[b], 80 * c[0] + 80 * (c[1] // 2 + 1))
                previous(dve, e_agg_t, c, after)
                dve.tensor_tensor(half_sum[:, b, 1, 0:n], parts[:, b, 2, 0:n], parts[:, b, 3, 0:n], ALU.add
                                  ).then_inc(e_half_b, 1)
                dve.wait_ge(e_exp, after(c))
                dve.tensor_scalar(soft[:, b, 0:n], soft[:, b, 0:n], EXP_MAX, None, ALU.min).then_inc(e_clamp, 1)
                dve.wait_ge(e_ln, after(c))
                previous(dve, e_out, c, after)
                dve.scalar_tensor_tensor(hidden[:, b, 0:n], pre_psum[:, b, 0:n], b_o1[:, 0:1], soft[:, b, 0:n],
                                         ALU.add, ALU.max).then_inc(e_hidden, 1)
                dve.wait_ge(e_out, after(c))
                previous(dve, e_kept, c, after)
                dve.tensor_tensor(y_rows[:, b, 0:n], total_psum[:, b, 0:n], x_rows[:, b, 0:n], ALU.add
                                  ).then_inc(e_row, 1)
                dve.wait_ge(e_row, after(c))
                for k in range(tiles):
                    last = dve.bn_stats(stats[:, b, k, :], y_rows[:, b, k * DIM:(k + 1) * DIM])
                last.then_inc(e_stats, 1)
                dve.wait_ge(flag_made, 1)
                dve.wait_ge(e_stats, after(c))
                for k in range(tiles):
                    last = dve.bn_aggr(chunk_mean_var[:, b, k, :], stats[:, b, k, :])
                last.then_inc(e_aggr, 1)
                dve.wait_ge(e_aggr, after(c))
                dve.tensor_copy(mean_var[:, bass.ds(first, tiles), :], chunk_mean_var[:, b, 0:tiles, :]
                                ).then_inc(e_moments, 1)

            run_chunks(dve, chunk, LAST_OUT)
            dve.wait_ge(e_kept, FULL_CHUNKS + 1)
            dve.wait_ge(e_dev, 1)
            dve.reciprocal(inv_dev[:, :], deviation[:, :]).then_inc(e_inv, 1)
            dve.wait_ge(e_inv, 1)
            dve.wait_ge(e_moments, FULL_CHUNKS + 1)
            for k in range(NODE_ROWS // P):
                d = slice(k * DIM, (k + 1) * DIM)
                dve.tensor_scalar(rows[:, d], rows[:, d], mean_var[:, k, 0:1], inv_dev[:, k:k + 1],
                                  ALU.subtract, ALU.mult).then_inc(e_norm, 1)

        @block.tensor
        def _(pe):
            pe.wait_ge(consts_loaded, 16 * 9)
            pe.wait_ge(consts_made, 7)
            pe.matmul(total_psum[:, 0, 0:DIM], minus_ln2[:, :], w_f2[:, :], start=True, stop=True)
            pe.matmul(total_psum[:, 0, DIM:2 * DIM], minus_ln2[:, :], w_o2[:, :], start=True, stop=True
                      ).then_inc(bias_mm, 1)

            def node_features(c, tiles):
                b = c[1] % 2
                pe.wait_ge(x_t_loaded[b], landed(c))
                previous(pe, h_left, c, after)
                x3 = x_t[:, b, 0:tiles * P].rearrange("d (p k) -> d k p", k=tiles)
                for k in range(tiles):
                    last = pe.matmul(pre_psum[:, b, k * DIM:(k + 1) * DIM], x3[:, k, :], w_in[:, :],
                                     start=True, stop=True)
                last.then_inc(h_mm, 1)

            run_chunks(pe, node_features, LAST_H)
            pe.wait_ge(bias_made, 6)
            pe.wait_ge(h_left, FULL_CHUNKS + 1)
            pe.wait_ge(flag_made, 1)
            is_narrow = pe.value_load(narrow[0:1, 0:1], min_val=0, max_val=1)

            def first_layer(g):
                b = g[1] % 2
                pe.wait_ge(f_loaded[b], landed(g))
                previous(pe, hidden_done, g, after)
                pe.matmul(pre_psum[:, b, :], w_f1[:, :], f_t[:, b, :], start=True, stop=True).then_inc(pre_done, 1)

            def second_layer(g):
                b = g[1] % 2
                pe.wait_ge(hidden_done, after(g))
                previous(pe, message_done, g, after)
                pe.matmul(filter_psum[:, b, :], ones_bias[:, :], bias_f[:, :, :].rearrange("q k d -> q (k d)"),
                          start=True, stop=False)
                for k in range(TILES):
                    d = slice(k * DIM, (k + 1) * DIM)
                    last = pe.matmul(filter_psum[:, b, d], hidden[:, b, k * P:(k + 1) * P], w_f2[:, :],
                                     start=False, stop=(k == TILES - 1))
                last.then_inc(filter_done, 1)

            def sum_repeated(g):
                b = g[1] % 2
                pe.wait_ge(message_done, after(g))
                pe.wait_ge(same_done, after(g))
                previous(pe, total_done, g, after)
                for k in range(TILES):
                    d = slice(k * DIM, (k + 1) * DIM)
                    last = pe.matmul(total_psum[:, b, d], same[:, b, k * P:(k + 1) * P], message[:, b, d],
                                     start=True, stop=True)
                last.then_inc(total_mm_done, 1)

            def gather(g):
                b = g[1] % 2
                pe.wait_ge(pick_done, after(g))
                pe.wait_ge(window_loaded[b], landed(g))
                previous(pe, h_dst_done, g, after)
                for k in range(TILES):
                    for part in range(3):
                        last = pe.matmul(gather_psum[:, b, k * DIM:(k + 1) * DIM], pick[:, b, k * P:(k + 1) * P],
                                         window[:, b, part, :], start=(part == 0), stop=(part == 2))
                last.then_inc(gather_done, 1)

            def step(i, narrow_form):
                if exists(plus(i, 2)):
                    first_layer(plus(i, 2))
                if exists(i):
                    second_layer(i)
                if exists(plus(i, -1)):
                    sum_repeated(plus(i, -1))
                if narrow_form and exists(plus(i, 1)):
                    gather(plus(i, 1))

            with pe.If(is_narrow):
                run_groups(pe, lambda i: step(i, True), -2)
            with pe.Else():
                run_groups(pe, lambda i: step(i, False), -2)

            pe.wait_ge(total_done, GROUPS)
            pe.wait_ge(message_done, GROUPS)

            def chunk(c, tiles):
                b, n = c[1] % 2, tiles * P
                pe.wait_ge(e_half_a, after(c))
                pe.wait_ge(e_half_b, after(c))
                previous(pe, e_agg_sb, c, after)
                for k in range(tiles):
                    d = slice(k * DIM, (k + 1) * DIM)
                    for s in range(2):
                        last = pe.matmul(filter_psum[:, b, d], half_sum[:, b, s, d], ident[:, :],
                                         start=(s == 0), stop=(s == 1))
                last.then_inc(e_agg_t, 1)
                pe.wait_ge(e_agg_sb, after(c))
                previous(pe, e_hidden, c, after)
                pe.matmul(pre_psum[:, b, 0:n], w_o1[:, :], agg_t[:, b, 0:n], start=True, stop=True).then_inc(e_pre, 1)
                pe.wait_ge(e_hidden, after(c))
                previous(pe, e_row, c, after)
                pe.matmul(total_psum[:, b, 0:n], ones_bias[:, :],
                          bias_o[:, 0:tiles, :].rearrange("q k d -> q (k d)"), start=True, stop=False)
                for k in range(tiles):
                    d = slice(k * DIM, (k + 1) * DIM)
                    last = pe.matmul(total_psum[:, b, d], hidden[:, b, k * P:(k + 1) * P], w_o2[:, :],
                                     start=False, stop=(k == tiles - 1))
                last.then_inc(e_out, 1)

            run_chunks(pe, chunk, LAST_OUT)


def kernel(x, src, dst, edge_attr_20, edge_weight, L0_gnn_W_in2f, L0_gnn_W_filt1, L0_gnn_b_filt1, L0_gnn_W_filt2,
           L0_gnn_b_filt2, L0_gnn_W_out1, L0_gnn_b_out1, L0_gnn_W_out2, L0_gnn_b_out2):
    import concourse.bacc as bacc
    from concourse.bass_utils import run_bass_kernel_spmd

    extra = EDGES_PAD - EDGES
    src_p = np.concatenate([np.asarray(src), np.full(extra, PAD_SRC, np.int32)])
    dst_p = np.pad(np.asarray(dst), (0, extra), mode="edge")

    def columns(a):
        return np.ascontiguousarray(a.reshape(GROUPS * TILES, P).T)

    def filled(a, n):
        return np.pad(np.asarray(a), ((0, n - a.shape[0]), (0, 0)))

    arrays = {
        "x": filled(x, NODE_ROWS),
        "x_t": np.ascontiguousarray(filled(x, WINDOW_ROWS).T),
        "f_t": np.ascontiguousarray(filled(edge_attr_20, EDGES_PAD).T),
        "src": src_p,
        "dst": dst_p,
        "src_cols": columns(src_p),
        "dst_cols": columns(dst_p),
        "weight_cols": columns(np.pad(np.asarray(edge_weight), (0, extra))),
        "w_in": L0_gnn_W_in2f, "w_f1": L0_gnn_W_filt1, "b_f1": L0_gnn_b_filt1,
        "w_f2": L0_gnn_W_filt2, "b_f2": L0_gnn_b_filt2, "w_o1": L0_gnn_W_out1,
        "b_o1": L0_gnn_b_out1, "w_o2": L0_gnn_W_out2, "b_o2": L0_gnn_b_out2,
    }
    arrays = {f"in_{n}": np.ascontiguousarray(a) for n, a in arrays.items()}
    nc = bacc.Bacc("TRN2", target_bir_lowering=False, num_devices=1)
    t = {n[3:]: nc.dram_tensor(n, a.shape, mybir.dt.from_np(a.dtype), kind="ExternalInput").ap()
         for n, a in arrays.items()}
    t["out"] = nc.dram_tensor("out", (NODES, DIM), F32, kind="ExternalOutput").ap()
    build(nc, t)
    return run_bass_kernel_spmd(nc, [arrays], core_ids=[0]).results[0]["out"]
```

```python
import math
from contextlib import ExitStack

import concourse.bass as bass
import numpy as np
from concourse import mybir
from concourse.alu_op_type import AluOpType as ALU

P = 128
NODES, DIM, RBF = 6250, 128, 20
EDGES = 200000
TILES = 4
GROUP = TILES * P
GROUPS = -(-EDGES // GROUP)
SLOTS = GROUPS + GROUPS % 2
EDGES_PAD = SLOTS * GROUP
CHUNK = 4 * P
FULL_CHUNKS = NODES // CHUNK
NODE_ROWS = -(-NODES // P) * P
TABLE_ROWS = NODE_ROWS + P
WINDOW_ROWS = TABLE_ROWS
LAST_H = WINDOW_ROWS - FULL_CHUNKS * CHUNK
LAST_OUT = NODE_ROWS - FULL_CHUNKS * CHUNK
PAD_SRC = NODES
GROUP_PARTS = 98
PER_PART = SLOTS // GROUP_PARTS
COLS = 13
LN2 = math.log(2.0)
EXP_ARG_MAX = 41.0
EPS = 1e-5
BIAS_ROWS = 96
FILL = 3
PAIRS = (GROUPS - 3 - FILL) // 2
CHUNKS = FULL_CHUNKS + 1
CHUNK_FILL = 4
CHUNK_PAIRS = (FULL_CHUNKS - 2 - CHUNK_FILL) // 2
FIFTHS = 5
LAST_ZEROS = {-2: (0, 1), -1: (2, 3), 0: (4,)}
ZEROED = 16 * FIFTHS * TILES

assert GROUP_PARTS * PER_PART == SLOTS and LAST_OUT == P and LAST_H == 2 * P
assert TABLE_ROWS % (FIFTHS * P) == 0 and FULL_CHUNKS // 2 - 1 == FIFTHS

F32, BF16 = mybir.dt.float32, mybir.dt.bfloat16
I32, U16 = mybir.dt.int32, mybir.dt.uint16
ACT = mybir.ActivationFunctionType
AX_X = mybir.AxisListType.X



def number(g):
    return 2 * g[0] + g[1]


def after(g):
    return 2 * g[0] + (g[1] + 1)


def landed(g):
    return 16 * g[0] + 16 * (g[1] // 2 + 1)


def scattered(g):
    return 32 * g[0] + 16 * (g[1] + 1)


def plus(g, n):
    return g[0], g[1] + n


def exists(g, n=GROUPS):
    return not isinstance(g[0], int) or 0 <= g[1] < n


def preloaded(g):
    return isinstance(g[0], int) and g[1] < 2


def is_last(c):
    return isinstance(c[0], int) and c[1] == CHUNKS - 1


def tiles_of(c):
    return LAST_OUT // P if is_last(c) else CHUNK // P


def build(nc, t):
    with ExitStack() as ctx:
        def sb(name, shape, dt):
            return ctx.enter_context(nc.sbuf_tensor(name, shape, dt))

        def sem(name):
            return ctx.enter_context(nc.semaphore(name))

        def dram(name, shape, dt):
            return nc.dram_tensor(name, shape, dt, kind="Internal").ap()

        dst16 = dram("dst16", (EDGES_PAD,), U16)
        src16 = dram("src16", (EDGES_PAD,), U16)
        base_d = dram("window_base", (SLOTS,), F32)
        spread_d = dram("window_spread", (SLOTS,), F32)
        h_parts = dram("h_parts", (WINDOW_ROWS, 3 * DIM), BF16)
        tables = [dram(f"table{k}", (TABLE_ROWS, DIM), F32) for k in range(TILES)]

        ident = sb("ident", [P, P], F32)
        earlier = sb("earlier", [P, P], F32)
        row_id = sb("row_id", [P, 1], F32)
        spare_row = sb("spare_row", [P, 1], F32)
        minus_ln2 = sb("minus_ln2", [P, P], F32)
        ones_bias = sb("ones_bias", [BIAS_ROWS, P], BF16)
        w_in = sb("w_in", [P, DIM], F32)
        w_f1 = sb("w_f1", [RBF, DIM], F32)
        w_f2 = sb("w_f2", [P, DIM], F32)
        w_o1 = sb("w_o1", [P, DIM], F32)
        w_o2 = sb("w_o2", [P, DIM], F32)
        b_f1 = sb("b_f1", [P, 1], F32)
        b_o1 = sb("b_o1", [P, 1], F32)
        b_f2 = sb("b_f2", [P, DIM], F32)
        b_o2 = sb("b_o2", [P, DIM], F32)
        bias_tmp = sb("bias_tmp", [P, 2, 4, DIM], F32)
        bias_hi = sb("bias_hi", [P, 2, 3, DIM], BF16)
        bias_f = sb("bias_f", [BIAS_ROWS, TILES, DIM], BF16)
        bias_o = sb("bias_o", [BIAS_ROWS, TILES, DIM], BF16)

        edge_cols = sb("edge_cols", [P, SLOTS, COLS], F32)
        src_i = sb("src_i", [P, SLOTS * TILES], I32)
        weight_c = sb("weight_c", [P, SLOTS * TILES], F32)
        dst_g = sb("dst_g", [GROUP_PARTS, PER_PART, GROUP], I32)
        src_g = sb("src_g", [GROUP_PARTS, PER_PART, GROUP], I32)
        dst_g16 = sb("dst_g16", [GROUP_PARTS, PER_PART * GROUP], U16)
        src_g16 = sb("src_g16", [GROUP_PARTS, PER_PART * GROUP], U16)
        dst_low = sb("dst_low", [GROUP_PARTS, PER_PART], F32)
        dst_high = sb("dst_high", [GROUP_PARTS, PER_PART], F32)
        dst_spread = sb("dst_spread", [GROUP_PARTS, PER_PART], F32)
        base_all = sb("base_all", [P, SLOTS], F32)
        base_i = sb("base_i", [1, SLOTS], I32)
        spread_row = sb("spread_row", [1, SLOTS], F32)
        widest = sb("widest", [1, 1], F32)
        narrow = sb("narrow", [1, 1], I32)

        x_t = sb("x_t", [P, 2, CHUNK], F32)
        h_out = sb("h_out", [P, 2, 4, 3, DIM], BF16)
        h_rest = sb("h_rest", [P, 2, 4, DIM], F32)
        zeros = sb("zeros", [P, TABLE_ROWS // (FIFTHS * P) * DIM], F32)

        f_t = sb("f_t", [RBF, 2, GROUP], F32)
        dst_b = sb("dst_b", [P, 2, GROUP], U16)
        src_b = sb("src_b", [P, 2, GROUP], U16)
        window = sb("window", [P, 2, 3, DIM], BF16)
        cols = sb("cols", [P, 2, COLS], F32)
        soft = sb("soft", [P, 2, GROUP], F32)
        hidden = sb("hidden", [P, 2, GROUP], F32)
        pick = sb("pick", [P, 2, GROUP], BF16)
        h_dst = sb("h_dst", [P, 2, GROUP], F32)
        same = sb("same", [P, 2, GROUP], F32)
        n_same = sb("n_same", [P, 2, TILES], F32)
        moved = sb("moved", [P, 2, TILES], F32)
        row_of = sb("row_of", [P, 2, TILES], F32)
        index = sb("index", [P, 2, TILES], I32)
        message = sb("message", [P, 2, GROUP], F32)
        total = sb("total", [P, 2, GROUP], F32)
        dst_i = sb("dst_i", [P, 2, TILES], I32)
        h_rows = sb("h_rows", [P, 2, TILES, 3, DIM], BF16)
        h_sum = sb("h_sum", [P, 2, GROUP], F32)

        parts = sb("parts", [P, 2, TILES, CHUNK], F32)
        half_sum = sb("half_sum", [P, 2, 2, CHUNK], F32)
        agg_t = sb("agg_t", [P, 2, CHUNK], F32)
        x_rows = sb("x_rows", [P, NODE_ROWS // P * DIM], F32)
        y_rows = sb("y_rows", [P, 2, CHUNK], F32)
        stats = sb("stats", [P, 2, 4, 6], F32)
        mean_var = sb("mean_var", [P, 2, 4, 2], F32)
        ln_var = sb("ln_var", [P, 2, 4], F32)
        inv_dev = sb("inv_dev", [P, 2, 4], F32)
        out_rows = sb("out_rows", [P, 2, CHUNK], F32)
        eps_col = sb("eps_col", [P, 1], F32)

        pre_psum = ctx.enter_context(nc.psum_tensor("pre_psum", [P, 2, GROUP], F32))
        filter_psum = ctx.enter_context(nc.psum_tensor("filter_psum", [P, 2, GROUP], F32))
        gather_psum = ctx.enter_context(nc.psum_tensor("gather_psum", [P, 2, GROUP], F32))
        total_psum = ctx.enter_context(nc.psum_tensor("total_psum", [P, 2, GROUP], F32))

        dst_loaded, src_loaded = sem("dst_loaded"), sem("src_loaded")
        cols_loaded, consts_loaded = sem("cols_loaded"), sem("consts_loaded")
        zeros_made, tables_zeroed = sem("zeros_made"), sem("tables_zeroed")
        const_step, consts_made = sem("const_step"), sem("consts_made")
        dst16_made, src16_made, edges16_stored = sem("dst16_made"), sem("src16_made"), sem("edges16_stored")
        spans_made, spans_stored, spans_loaded = sem("spans_made"), sem("spans_stored"), sem("spans_loaded")
        dve_step = sem("dve_step")
        cols_made, window_cols_made, flag_made = sem("cols_made"), sem("window_cols_made"), sem("flag_made")
        bias_mm, bias_parts, bias_made = sem("bias_mm"), sem("bias_parts"), sem("bias_made")
        x_t_loaded = [sem(f"x_t_loaded{b}") for b in range(2)]
        h_mm, h_hi, h_left, h_mid, h_lo = (sem(n) for n in ("h_mm", "h_hi", "h_left", "h_mid", "h_lo"))
        h_stored = [sem(f"h_stored{b}") for b in range(2)]

        f_loaded = [sem(f"f_loaded{b}") for b in range(2)]
        dst_b_loaded = [sem(f"dst_b_loaded{b}") for b in range(2)]
        dst_i_loaded = [sem(f"dst_i_loaded{b}") for b in range(2)]
        src_b_loaded = [sem(f"src_b_loaded{b}") for b in range(2)]
        window_loaded = [sem(f"window_loaded{b}") for b in range(2)]
        pre_done, exp_done, clamp_done = sem("pre_done"), sem("exp_done"), sem("clamp_done")
        ln_done, hidden_done, filter_done = sem("ln_done"), sem("hidden_done"), sem("filter_done")
        cols_done, pick_done = sem("cols_done"), sem("pick_done")
        gather_done, h_dst_done = sem("gather_done"), sem("h_dst_done")
        same_done, moved_done = sem("same_done"), sem("moved_done")
        row_done, index_done = sem("row_done"), sem("index_done")
        message_done, total_mm_done, total_done = sem("message_done"), sem("total_mm_done"), sem("total_done")
        table_added = [sem(f"table_added{k}") for k in range(TILES)]
        rows_gathered = [sem(f"rows_gathered{b}") for b in range(2)]
        h_sum_step, pool_turns = sem("h_sum_step"), sem("pool_turns")

        x_rows_loaded = sem("x_rows_loaded")
        parts_loaded = [sem(f"parts_loaded{b}") for b in range(2)]
        e_halves, e_agg_t, e_agg_sb = sem("e_halves"), sem("e_agg_t"), sem("e_agg_sb")
        e_pre, e_clamp, e_exp, e_ln, e_hidden = (sem(n) for n in ("e_pre", "e_clamp", "e_exp", "e_ln", "e_hidden"))
        e_out, e_row, e_stats, e_aggr = sem("e_out"), sem("e_row"), sem("e_stats"), sem("e_aggr")
        e_ln_var, e_inv, e_norm = sem("e_ln_var"), sem("e_inv"), sem("e_norm")
        out_stored = [sem(f"out_stored{b}") for b in range(2)]

        block = ctx.enter_context(nc.Block())

        def run_groups(eng, step, first=-1):
            for i in range(first, FILL):
                step((0, i))
            with eng.Fori(0, PAIRS) as j:
                step((j, FILL))
                step((j, FILL + 1))
            for i in range(FILL + 2 * PAIRS, GROUPS + 1):
                step((0, i))

        def run_chunks(eng, step, last):
            step((0, 0), CHUNK // P)
            step((0, 1), CHUNK // P)
            with eng.Fori(0, FULL_CHUNKS // 2 - 1) as j:
                step((j, 2), CHUNK // P)
                step((j, 3), CHUNK // P)
            step((0, FULL_CHUNKS), last // P)

        def run_last_layers(eng, step):
            for i in range(-2, CHUNK_FILL):
                step((0, i))
            with eng.Fori(0, CHUNK_PAIRS) as j:
                step((j, CHUNK_FILL))
                step((j, CHUNK_FILL + 1))
            for i in range(CHUNK_FILL + 2 * CHUNK_PAIRS, CHUNKS + 3):
                step((0, i))

        def previous(eng, s, g, count, n=2):
            if not isinstance(g[0], int) or g[1] >= n:
                eng.wait_ge(s, count(plus(g, -n)))

        def held(eng, count, g):
            if isinstance(g[0], int):
                return count(g) if g[1] >= 0 else None
            return eng.snap(count(g))

        @block.sync
        def _(sp):
            def load_x_t(c, tiles):
                b, n = c[1] % 2, number(c)
                previous(sp, h_mm, c, after)
                sp.dma_start(x_t[:, b, 0:tiles * P], t["x_t"][:, bass.ds(n * CHUNK, tiles * P)]
                             ).then_inc(x_t_loaded[b], 16)

            def store_h(c, tiles):
                b, n = c[1] % 2, number(c)
                sp.wait_ge(h_lo, after(c))
                sp.dma_start(h_parts[bass.ds(n * CHUNK, tiles * P), :].rearrange("(p t) d -> p t d", t=tiles),
                             h_out[:, b, 0:tiles, :, :].rearrange("p t k d -> p t (k d)")
                             ).then_inc(h_stored[b], 16)

            sp.dma_start(dst_g[:, :, :], t["dst"].rearrange("(p g e) -> p g e", p=GROUP_PARTS, e=GROUP)
                         ).then_inc(dst_loaded, 16)
            load_x_t((0, 0), CHUNK // P)
            load_x_t((0, 1), CHUNK // P)
            sp.dma_start(src_g[:, :, :], t["src"].rearrange("(p g e) -> p g e", p=GROUP_PARTS, e=GROUP)
                         ).then_inc(src_loaded, 16)

            sp.wait_ge(spans_made, 2)
            sp.dma_start(base_d.rearrange("(p g) -> p g", p=GROUP_PARTS), dst_low[:, :]).then_inc(spans_stored, 16)
            sp.dma_start(spread_d.rearrange("(p g) -> p g", p=GROUP_PARTS), dst_spread[:, :]
                         ).then_inc(spans_stored, 16)
            sp.wait_ge(dst16_made, 1)
            sp.dma_start(dst16.rearrange("(p e) -> p e", p=GROUP_PARTS), dst_g16[:, :]).then_inc(edges16_stored, 16)
            sp.wait_ge(src16_made, 1)
            sp.dma_start(src16.rearrange("(p e) -> p e", p=GROUP_PARTS), src_g16[:, :]).then_inc(edges16_stored, 16)
            sp.wait_ge(spans_stored, 32)
            sp.dma_start(base_all[:, :], base_d.partition_broadcast(P)).then_inc(spans_loaded, 16)
            sp.dma_start(spread_row[:, :], spread_d.partition_broadcast(1)).then_inc(spans_loaded, 16)

            sp.dma_start(src_i[:, :], t["src_cols"]).then_inc(cols_loaded, 16)
            sp.dma_start(weight_c[:, :], t["weight_cols"]).then_inc(cols_loaded, 16)

            def load_features(g):
                b = g[1] % 2
                before = held(sp, after, plus(g, -2))
                sp.wait_ge(dst_loaded, 16)
                if before is not None:
                    sp.wait_ge(pre_done, before)
                sp.dma_start(f_t[:, b, :], t["f_t"][:, bass.ds(number(g) * GROUP, GROUP)]).then_inc(f_loaded[b], 16)

            def load_dst(g):
                b = g[1] % 2
                before = held(sp, after, plus(g, -2))
                sp.wait_ge(dst_loaded, 16)
                if before is not None:
                    sp.wait_ge(pick_done, before)
                sp.dma_start(dst_b[:, b, :], dst16[bass.ds(number(g) * GROUP, GROUP)].partition_broadcast(P)
                             ).then_inc(dst_b_loaded[b], 16)

            def load_src(g):
                b = g[1] % 2
                before = held(sp, after, plus(g, -2))
                sp.wait_ge(dst_loaded, 16)
                if before is not None:
                    sp.wait_ge(same_done, before)
                sp.dma_start(src_b[:, b, :], src16[bass.ds(number(g) * GROUP, GROUP)].partition_broadcast(P)
                             ).then_inc(src_b_loaded[b], 16)

            for g in ((0, 0), (0, 1)):
                load_features(g)
            sp.wait_ge(edges16_stored, 32)
            for g in ((0, 0), (0, 1)):
                load_src(g)

            with sp.Fori(0, FULL_CHUNKS // 2 - 1) as j:
                for b in range(2):
                    load_x_t((j, b + 2), CHUNK // P)
                    store_h((j, b), CHUNK // P)
            load_x_t((0, FULL_CHUNKS), LAST_H // P)
            store_h((0, FULL_CHUNKS - 2), CHUNK // P)
            store_h((0, FULL_CHUNKS - 1), CHUNK // P)
            store_h((0, FULL_CHUNKS), LAST_H // P)
            sp.wait_ge(flag_made, 1)
            is_narrow = sp.value_load(narrow[0:1, 0:1], min_val=0, max_val=1)

            def step_narrow(i):
                if exists(plus(i, 3)) and not preloaded(plus(i, 3)):
                    load_features(plus(i, 3))
                g = plus(i, 2)
                b = g[1] % 2
                if exists(g):
                    load_dst(g)
                    if isinstance(g[0], int) and g[1] == 0:
                        for k in range(2):
                            sp.wait_ge(h_stored[k], 16 * (FULL_CHUNKS // 2 + (k == 0)))
                    start = sp.value_load(base_i[0:1, bass.ds(number(g), 1)], min_val=0, max_val=NODES - 1)
                    previous(sp, gather_done, g, after)
                    sp.dma_start(window[:, b, :, :], h_parts[bass.ds(start, P), :].rearrange("n (k d) -> n k d", k=3)
                                 ).then_inc(window_loaded[b], 16)
                if exists(plus(i, 1)) and not preloaded(plus(i, 1)):
                    load_src(plus(i, 1))

            def step_general(i):
                if exists(plus(i, 3)) and not preloaded(plus(i, 3)):
                    load_features(plus(i, 3))
                g = plus(i, 2)
                b = g[1] % 2
                if exists(g):
                    if not isinstance(g[0], int) or g[1] >= 2:
                        sp.wait_ge(rows_gathered[b], 64 * g[0] + 64 * (g[1] // 2))
                    sp.dma_start(dst_i[:, b, :], t["dst_cols"][:, bass.ds(number(g) * TILES, TILES)]
                                 ).then_inc(dst_i_loaded[b], 16)
                if exists(plus(i, 1)) and not preloaded(plus(i, 1)):
                    load_src(plus(i, 1))

            with sp.If(is_narrow):
                run_groups(sp, step_narrow, -3)
            with sp.Else():
                run_groups(sp, step_general, -3)

            full = FULL_CHUNKS * CHUNK
            sp.dma_start(x_rows[:, 0:full // P * DIM].rearrange("p (c t d) -> p c t d", t=4, d=DIM),
                         t["x"][0:full, :].rearrange("(c p t) d -> p c t d", p=P, t=4)).then_inc(x_rows_loaded, 16)
            sp.dma_start(x_rows[:, full // P * DIM:NODE_ROWS // P * DIM], t["x"][full:NODE_ROWS, :]
                         ).then_inc(x_rows_loaded, 16)

            def load_tables(c):
                b, tiles = c[1] % 2, tiles_of(c)
                previous(sp, e_halves, c, lambda g: 2 * after(g))
                for k in range(TILES):
                    if isinstance(c[0], int) and c[1] == 0:
                        sp.wait_ge(table_added[k], 16 * GROUPS)
                    sp.dma_start(parts[:, b, k, 0:tiles * DIM].rearrange("p (t d) -> p t d", d=DIM),
                                 tables[k][bass.ds(number(c) * CHUNK, tiles * P), :]
                                 .rearrange("(p t) d -> p t d", t=tiles)).then_inc(parts_loaded[b], 16)

            def last_layers(i):
                if exists(plus(i, 2), CHUNKS):
                    load_tables(plus(i, 2))

            run_last_layers(sp, last_layers)

        @block.gpsimd
        def _(pool):
            pool.memset(zeros[:, :], 0.0).then_inc(zeros_made, 1)
            pool.memset(earlier[:, :], 1.0).then_inc(const_step, 1)
            pool.memset(ident[:, :], 0.0).then_inc(const_step, 1)
            pool.memset(ones_bias[:, :], 1.0).then_inc(consts_made, 1)
            pool.memset(minus_ln2[:, :], -LN2).then_inc(consts_made, 1)
            pool.memset(eps_col[:, :], EPS).then_inc(consts_made, 1)
            pool.iota(row_id[:, :], pattern=[[0, 1]], base=0, channel_multiplier=1,
                      allow_small_or_imprecise_dtypes=True).then_inc(consts_made, 1)
            pool.iota(spare_row[:, :], pattern=[[0, 1]], base=NODE_ROWS, channel_multiplier=1,
                      allow_small_or_imprecise_dtypes=True).then_inc(consts_made, 1)
            pool.wait_ge(const_step, 2)
            pool.affine_select(out=earlier[:, :], in_=earlier[:, :], compare_op=ALU.is_ge, fill=0.0, base=0,
                               pattern=[[-1, P]], channel_multiplier=1).then_inc(consts_made, 1)
            pool.affine_select(out=ident[:, :], in_=ident[:, :], compare_op=ALU.not_equal, fill=1.0, base=0,
                               pattern=[[-1, P]], channel_multiplier=1).then_inc(consts_made, 1)

            def grouped(x):
                return x.rearrange("p (g k) -> p g k", k=TILES)

            pool.wait_ge(cols_loaded, 32)
            pool.wait_ge(consts_made, 7)
            pool.tensor_copy(edge_cols[:, :, 0:4], grouped(src_i[:, :])).then_inc(cols_made, 1)
            pool.tensor_copy(edge_cols[:, :, 4:8], grouped(weight_c[:, :])).then_inc(cols_made, 1)
            pool.tensor_scalar(edge_cols[:, :, 8:12], grouped(src_i[:, :]), -1.0, spare_row[:, 0:1],
                               ALU.mult, ALU.add).then_inc(cols_made, 1)

            pool.wait_ge(flag_made, 1)
            is_narrow = pool.value_load(narrow[0:1, 0:1], min_val=0, max_val=1)

            def scatter(g):
                b = g[1] % 2
                before = held(pool, scattered, plus(g, -1))
                pool.wait_ge(index_done, after(g))
                pool.wait_ge(total_done, after(g))
                if before is not None:
                    pool.wait_ge(table_added[0], before)
                pool.sem_inc(pool_turns, 1)
                for k in range(TILES):
                    pool.wait_ge(tables_zeroed, ZEROED)
                    if before is not None and k:
                        pool.wait_ge(table_added[k], before)
                    pool.indirect_dma_start(tables[k], bass.IndirectOffsetOnAxis(index[:, b, k:k + 1], 0),
                                            total[:, b, k * DIM:(k + 1) * DIM], None, compute_op=ALU.add
                                            ).then_inc(table_added[k], 16)

            def gather(g):
                b = g[1] % 2
                arrived = held(pool, landed, g)
                before = held(pool, after, plus(g, -2))
                pool.wait_ge(dst_i_loaded[b], arrived)
                if before is not None:
                    pool.wait_ge(h_dst_done, before)
                pool.sem_inc(pool_turns, 1)
                for k in range(TILES):
                    pool.indirect_dma_start(h_rows[:, b, k, :, :].rearrange("p k d -> p (k d)"), None, h_parts,
                                            bass.IndirectOffsetOnAxis(dst_i[:, b, k:k + 1], 0)
                                            ).then_inc(rows_gathered[b], 16)

            def step_narrow(i):
                if exists(plus(i, -1)):
                    scatter(plus(i, -1))

            def step_general(i):
                if exists(plus(i, 1)):
                    gather(plus(i, 1))
                if exists(plus(i, -1)):
                    scatter(plus(i, -1))

            with pool.If(is_narrow):
                run_groups(pool, step_narrow)
            with pool.Else():
                for b in range(2):
                    pool.wait_ge(h_stored[b], 16 * (FULL_CHUNKS // 2 + (b == 0)))
                run_groups(pool, step_general)

            def last_layers(i):
                c = plus(i, 1)
                if exists(c, CHUNKS):
                    b, n = c[1] % 2, tiles_of(c) * DIM
                    pool.wait_ge(parts_loaded[b], 64 * c[0] + 64 * (c[1] // 2 + 1))
                    previous(pool, e_agg_t, c, after)
                    for s in range(2):
                        pool.tensor_tensor(half_sum[:, b, s, 0:n], parts[:, b, 2 * s, 0:n], parts[:, b, 2 * s + 1, 0:n],
                                           ALU.add).then_inc(e_halves, 1)

            run_last_layers(pool, last_layers)

        @block.scalar
        def _(act):
            for dest, name in ((w_in, "w_in"), (w_f2, "w_f2"), (w_o2, "w_o2")):
                act.dma_start(dest[:, :], t[name]).then_inc(consts_loaded, 16)
            for dest, name in ((b_f2, "b_f2"), (b_o2, "b_o2")):
                act.dma_start(dest[:, :], t[name].partition_broadcast(P)).then_inc(consts_loaded, 16)

            def zero(k, fifth):
                rows = bass.ds(fifth * (TABLE_ROWS // FIFTHS), TABLE_ROWS // FIFTHS)
                act.dma_start(tables[k][rows, :].rearrange("(p r) d -> p (r d)", p=P), zeros[:, :]
                              ).then_inc(tables_zeroed, 16)

            for dest, name in ((w_f1, "w_f1"), (w_o1, "w_o1")):
                act.dma_start(dest[:, :], t[name]).then_inc(consts_loaded, 16)
            for dest, name in ((b_f1, "b_f1"), (b_o1, "b_o1")):
                act.dma_start(dest[:, :], t[name].rearrange("(p a) -> p a", a=1)).then_inc(consts_loaded, 16)
            act.wait_ge(zeros_made, 1)
            for fifth in range(2):
                zero(0, fifth)

            act.preload_act_table_set("natural_log_exp_and_others")

            def split_h(c, tiles):
                b = c[1] % 2
                if not isinstance(c[0], int):
                    zero(1 + b, c[0])
                else:
                    zero(0, min(2 + c[1], FIFTHS - 1))
                act.wait_ge(h_mm, after(c))
                previous(act, h_stored[b], c, landed)
                act.activation(h_out[:, b, 0:tiles, 0, :],
                               pre_psum[:, b, 0:tiles * DIM].rearrange("p (t d) -> p t d", d=DIM), ACT.Copy
                               ).then_inc(h_hi, 1)
                act.wait_ge(h_left, after(c))
                act.activation(h_out[:, b, 0:tiles, 1, :], h_rest[:, b, 0:tiles, :], ACT.Copy).then_inc(h_mid, 1)

            run_chunks(act, split_h, LAST_H)
            act.wait_ge(consts_loaded, 16 * 9)
            act.wait_ge(consts_made, 7)
            act.wait_ge(flag_made, 1)
            is_narrow = act.value_load(narrow[0:1, 0:1], min_val=0, max_val=1)
            act.wait_ge(cols_made, 3)
            act.wait_ge(window_cols_made, 1)

            def exponential(g):
                b = g[1] % 2
                act.wait_ge(clamp_done, after(g))
                act.activation(soft[:, b, :], soft[:, b, :], ACT.Exp).then_inc(exp_done, 1)

            def columns(g):
                b = g[1] % 2
                previous(act, row_done, g, after)
                previous(act, h_dst_done, g, after)
                act.activation(cols[:, b, :], edge_cols[:, bass.ds(number(g), 1), :].rearrange("p a c -> p (a c)"),
                               ACT.Copy).then_inc(cols_done, 1)

            def logarithm(g):
                b = g[1] % 2
                act.wait_ge(exp_done, after(g))
                act.activation(soft[:, b, :], soft[:, b, :], ACT.Ln, bias=1.0).then_inc(ln_done, 1)

            def copy_total(g):
                b = g[1] % 2
                act.wait_ge(total_mm_done, after(g))
                for k in range(TILES):
                    previous(act, table_added[k], g, scattered)
                act.activation(total[:, b, :], total_psum[:, b, :], ACT.Copy).then_inc(total_done, 1)

            def weigh_h_dst(g, narrow_form):
                b = g[1] % 2
                if narrow_form:
                    act.wait_ge(gather_done, after(g))
                else:
                    act.wait_ge(h_sum_step, 2 * after(g))
                act.wait_ge(cols_done, after(g))
                previous(act, message_done, g, after)
                for k in range(TILES):
                    d = slice(k * DIM, (k + 1) * DIM)
                    source = gather_psum if narrow_form else h_sum
                    last = act.activation(h_dst[:, b, d], source[:, b, d], ACT.Copy, scale=cols[:, b, 4 + k:5 + k])
                last.then_inc(h_dst_done, 1)

            def step(i, narrow_form):
                if exists(plus(i, 1)):
                    exponential(plus(i, 1))
                    logarithm(plus(i, 1))
                if isinstance(i[0], int) and i[1] in LAST_ZEROS:
                    for fifth in LAST_ZEROS[i[1]]:
                        zero(TILES - 1, fifth)
                if exists(plus(i, -1)):
                    copy_total(plus(i, -1))
                if not narrow_form and exists(i):
                    weigh_h_dst(i, False)
                if exists(plus(i, 2)):
                    columns(plus(i, 2))
                if narrow_form and exists(plus(i, 1)):
                    weigh_h_dst(plus(i, 1), True)

            with act.If(is_narrow):
                run_groups(act, lambda i: step(i, True), -2)
            with act.Else():
                run_groups(act, lambda i: step(i, False), -2)

            def store_rows(c):
                b = c[1] % 2
                act.wait_ge(e_norm, after(c))
                if is_last(c):
                    full = FULL_CHUNKS * CHUNK
                    act.dma_start(t["out"][full:NODES, :], out_rows[0:NODES - full, b, 0:DIM]
                                  ).then_inc(out_stored[b], 16)
                else:
                    act.dma_start(t["out"][bass.ds(number(c) * CHUNK, CHUNK), :].rearrange("(p t) d -> p t d", t=4),
                                  out_rows[:, b, :].rearrange("p (t d) -> p t d", d=DIM)).then_inc(out_stored[b], 16)

            def last_layers(i):
                if exists(plus(i, -3), CHUNKS):
                    store_rows(plus(i, -3))
                c = plus(i, 1)
                if exists(c, CHUNKS):
                    b, n = c[1] % 2, tiles_of(c) * P
                    act.wait_ge(e_agg_t, after(c))
                    previous(act, e_pre, c, after)
                    act.activation(agg_t[:, b, 0:n], filter_psum[:, b, 0:n], ACT.Copy).then_inc(e_agg_sb, 1)
                c = i
                if exists(c, CHUNKS):
                    b, n = c[1] % 2, tiles_of(c) * P
                    act.wait_ge(e_clamp, after(c))
                    act.activation(soft[:, b, 0:n], soft[:, b, 0:n], ACT.Exp).then_inc(e_exp, 1)
                    act.wait_ge(e_exp, after(c))
                    act.activation(soft[:, b, 0:n], soft[:, b, 0:n], ACT.Ln, bias=1.0).then_inc(e_ln, 1)
                c = plus(i, -1)
                if exists(c, CHUNKS):
                    b, tiles = c[1] % 2, tiles_of(c)
                    act.wait_ge(e_aggr, after(c))
                    previous(act, e_inv, c, after)
                    act.activation(ln_var[:, b, 0:tiles], mean_var[:, b, 0:tiles, 1], ACT.Ln, bias=eps_col[:, 0:1]
                                   ).then_inc(e_ln_var, 1)
                    act.wait_ge(e_ln_var, after(c))
                    previous(act, e_norm, c, after)
                    act.activation(inv_dev[:, b, 0:tiles], ln_var[:, b, 0:tiles], ACT.Exp, scale=-0.5
                                   ).then_inc(e_inv, 1)

            run_last_layers(act, last_layers)
            for b in range(2):
                act.wait_ge(out_stored[b], landed((0, CHUNKS - 1 - (CHUNKS - 1 - b) % 2)))

        @block.vector
        def _(dve):
            dve.wait_ge(dst_loaded, 16)
            dve.tensor_reduce(dst_low[:, :], dst_g[:, :, :], AX_X, ALU.min).then_inc(spans_made, 1)
            dve.tensor_reduce(dst_high[:, :], dst_g[:, :, :], AX_X, ALU.max).then_inc(dve_step, 1)
            dve.wait_ge(spans_made, 1)
            dve.wait_ge(dve_step, 1)
            dve.tensor_tensor(dst_spread[:, :], dst_high[:, :], dst_low[:, :], ALU.subtract).then_inc(spans_made, 1)
            dve.tensor_copy(dst_g16[:, :], dst_g[:, :, :].rearrange("p g e -> p (g e)")).then_inc(dst16_made, 1)
            dve.wait_ge(src_loaded, 16)
            dve.tensor_copy(src_g16[:, :], src_g[:, :, :].rearrange("p g e -> p (g e)")).then_inc(src16_made, 1)

            def make_biases():
                dve.wait_ge(consts_loaded, 16 * 9)
                dve.wait_ge(bias_mm, 1)
                dve.tensor_tensor(bias_tmp[:, 0, 0, :], total_psum[:, 0, 0:DIM], b_f2[:, :], ALU.add
                                  ).then_inc(dve_step, 1)
                dve.tensor_tensor(bias_tmp[:, 1, 0, :], total_psum[:, 0, DIM:2 * DIM], b_o2[:, :], ALU.add
                                  ).then_inc(dve_step, 1)
                steps = 5
                for part in range(3):
                    dve.wait_ge(dve_step, steps)
                    dve.tensor_copy(bias_hi[:, :, part, :], bias_tmp[:, :, part, :]).then_inc(dve_step, 1)
                    steps += 1
                    if part < 2:
                        dve.wait_ge(dve_step, steps)
                        dve.tensor_tensor(bias_tmp[:, :, part + 1, :], bias_tmp[:, :, part, :], bias_hi[:, :, part, :],
                                          ALU.subtract).then_inc(dve_step, 1)
                        steps += 1
                dve.memset(bias_f[:, :, :], 0.0).then_inc(dve_step, 1)
                dve.memset(bias_o[:, :, :], 0.0).then_inc(dve_step, 1)
                dve.wait_ge(dve_step, steps + 2)
                for which, dest in enumerate((bias_f, bias_o)):
                    for part in range(3):
                        q = 32 * part
                        dve.tensor_copy(dest[q:q + 1, :, :], bias_hi[q:q + 1, which:which + 1, part, :]
                                        .to_broadcast([1, TILES, DIM])).then_inc(bias_made, 1)

            def judge_windows():
                dve.wait_ge(spans_loaded, 32)
                dve.wait_ge(consts_made, 7)
                dve.tensor_scalar(edge_cols[:, :, 12], base_all[:, :], row_id[:, 0:1], None, ALU.add
                                  ).then_inc(window_cols_made, 1)
                dve.tensor_copy(base_i[:, :], base_all[0:1, :]).then_inc(dve_step, 1)
                dve.tensor_reduce(widest[:, :], spread_row[:, :], AX_X, ALU.max).then_inc(dve_step, 1)
                dve.wait_ge(dve_step, 3)
                dve.tensor_scalar(narrow[:, :], widest[:, :], float(P) - 0.5, None, ALU.is_lt).then_inc(flag_made, 1)

            def split_h(c, tiles):
                b = c[1] % 2
                dve.wait_ge(h_hi, after(c))
                previous(dve, h_mid, c, after)
                dve.tensor_tensor(h_rest[:, b, 0:tiles, :],
                                  pre_psum[:, b, 0:tiles * DIM].rearrange("p (t d) -> p t d", d=DIM),
                                  h_out[:, b, 0:tiles, 0, :], ALU.subtract).then_inc(h_left, 1)
                dve.wait_ge(h_mid, after(c))
                dve.wait_ge(h_left, after(c))
                dve.tensor_tensor(h_out[:, b, 0:tiles, 2, :], h_rest[:, b, 0:tiles, :], h_out[:, b, 0:tiles, 1, :],
                                  ALU.subtract).then_inc(h_lo, 1)
                if isinstance(c[0], int) and c[1] == 1:
                    judge_windows()
                    make_biases()

            run_chunks(dve, split_h, LAST_H)
            dve.wait_ge(flag_made, 1)
            is_narrow = dve.value_load(narrow[0:1, 0:1], min_val=0, max_val=1)

            def compare_src(g):
                b = g[1] % 2
                dve.wait_ge(cols_done, after(g))
                dve.wait_ge(src_b_loaded[b], landed(g))
                previous(dve, total_mm_done, g, after)
                for k in range(TILES):
                    tile = slice(k * P, (k + 1) * P)
                    last = dve.scalar_tensor_tensor(same[:, b, tile], src_b[:, b, tile], cols[:, b, k:k + 1],
                                                    earlier[:, :], ALU.is_equal, ALU.mult,
                                                    accum_out=n_same[:, b, k:k + 1])
                last.then_inc(same_done, 1)

            def compare_dst(g):
                b = g[1] % 2
                dve.wait_ge(cols_done, after(g))
                dve.wait_ge(dst_b_loaded[b], landed(g))
                previous(dve, gather_done, g, after)
                dve.tensor_scalar(pick[:, b, :], dst_b[:, b, :], cols[:, b, 12:13], None, ALU.is_equal
                                  ).then_inc(pick_done, 1)

            def move_repeated(g):
                b = g[1] % 2
                dve.wait_ge(same_done, after(g))
                dve.scalar_tensor_tensor(moved[:, b, :], n_same[:, b, :], 1.5, cols[:, b, 8:12],
                                         ALU.is_gt, ALU.mult).then_inc(moved_done, 1)

            def add_src(g):
                b = g[1] % 2
                dve.wait_ge(moved_done, after(g))
                dve.tensor_tensor(row_of[:, b, :], moved[:, b, :], cols[:, b, 0:4], ALU.add).then_inc(row_done, 1)

            def make_index(g):
                b = g[1] % 2
                dve.wait_ge(row_done, after(g))
                for k in range(TILES):
                    previous(dve, table_added[k], g, scattered)
                dve.tensor_copy(index[:, b, :], row_of[:, b, :]).then_inc(index_done, 1)

            def clamp(g):
                b = g[1] % 2
                dve.wait_ge(pre_done, after(g))
                previous(dve, hidden_done, g, after)
                dve.tensor_scalar(soft[:, b, :], pre_psum[:, b, :], b_f1[:, 0:1], EXP_ARG_MAX, ALU.add, ALU.min
                                  ).then_inc(clamp_done, 1)

            def finish_hidden(g):
                b = g[1] % 2
                dve.wait_ge(ln_done, after(g))
                previous(dve, filter_done, g, after)
                dve.scalar_tensor_tensor(hidden[:, b, :], pre_psum[:, b, :], b_f1[:, 0:1], soft[:, b, :],
                                         ALU.add, ALU.max).then_inc(hidden_done, 1)

            def sum_parts(g):
                b = g[1] % 2
                dve.wait_ge(rows_gathered[b], 64 * g[0] + 64 * (g[1] // 2 + 1))
                h3 = h_sum[:, b, :].rearrange("p (k d) -> p k d", d=DIM)
                previous(dve, h_dst_done, g, after)
                dve.tensor_tensor(h3, h_rows[:, b, :, 0, :], h_rows[:, b, :, 1, :], ALU.add).then_inc(h_sum_step, 1)
                dve.wait_ge(h_sum_step, 2 * number(g) + 1)
                dve.tensor_tensor(h3, h3, h_rows[:, b, :, 2, :], ALU.add).then_inc(h_sum_step, 1)

            def multiply(g):
                b = g[1] % 2
                dve.wait_ge(filter_done, after(g))
                dve.wait_ge(h_dst_done, after(g))
                previous(dve, total_mm_done, g, after)
                dve.tensor_tensor(message[:, b, :], filter_psum[:, b, :], h_dst[:, b, :], ALU.mult
                                  ).then_inc(message_done, 1)

            def step(i, narrow_form):
                if exists(plus(i, 1)) and narrow_form:
                    compare_dst(plus(i, 1))
                if exists(plus(i, 1)):
                    clamp(plus(i, 1))
                if exists(i):
                    compare_src(i)
                if exists(plus(i, -1)):
                    make_index(plus(i, -1))
                if exists(i):
                    move_repeated(i)
                    add_src(i)
                if exists(plus(i, 1)):
                    finish_hidden(plus(i, 1))
                if exists(i):
                    if not narrow_form:
                        sum_parts(i)
                    multiply(i)

            with dve.If(is_narrow):
                run_groups(dve, lambda i: step(i, True))
            with dve.Else():
                run_groups(dve, lambda i: step(i, False))

            def last_layers(i):
                c = i
                if exists(c, CHUNKS):
                    b, n = c[1] % 2, tiles_of(c) * P
                    dve.wait_ge(e_pre, after(c))
                    previous(dve, e_hidden, c, after)
                    dve.tensor_scalar(soft[:, b, 0:n], pre_psum[:, b, 0:n], b_o1[:, 0:1], EXP_ARG_MAX,
                                      ALU.add, ALU.min).then_inc(e_clamp, 1)
                c = plus(i, -2)
                if exists(c, CHUNKS):
                    b, tiles = c[1] % 2, tiles_of(c)
                    dve.wait_ge(e_inv, after(c))
                    previous(dve, out_stored[b], c, landed)
                    for k in range(tiles):
                        d = slice(k * DIM, (k + 1) * DIM)
                        last = dve.tensor_scalar(out_rows[:, b, d], y_rows[:, b, d], mean_var[:, b, k, 0:1],
                                                 inv_dev[:, b, k:k + 1], ALU.subtract, ALU.mult)
                    last.then_inc(e_norm, 1)
                c = plus(i, -1)
                if exists(c, CHUNKS):
                    b, tiles = c[1] % 2, tiles_of(c)
                    n = tiles * DIM
                    dve.wait_ge(e_out, after(c))
                    previous(dve, e_norm, c, after)
                    dve.tensor_tensor(y_rows[:, b, 0:n], total_psum[:, b, 0:n],
                                      x_rows[:, bass.ds(number(c) * CHUNK, n)], ALU.add).then_inc(e_row, 1)
                    dve.wait_ge(e_row, after(c))
                    for k in range(tiles):
                        last = dve.bn_stats(stats[:, b, k, :], y_rows[:, b, k * DIM:(k + 1) * DIM])
                    last.then_inc(e_stats, 1)
                    dve.wait_ge(flag_made, 1)
                    dve.wait_ge(e_stats, after(c))
                    for k in range(tiles):
                        last = dve.bn_aggr(mean_var[:, b, k, :], stats[:, b, k, :])
                    last.then_inc(e_aggr, 1)
                c = i
                if exists(c, CHUNKS):
                    b, n = c[1] % 2, tiles_of(c) * P
                    dve.wait_ge(e_ln, after(c))
                    previous(dve, e_out, c, after)
                    dve.scalar_tensor_tensor(hidden[:, b, 0:n], pre_psum[:, b, 0:n], b_o1[:, 0:1], soft[:, b, 0:n],
                                             ALU.add, ALU.max).then_inc(e_hidden, 1)

            dve.wait_ge(x_rows_loaded, 32)
            run_last_layers(dve, last_layers)

        @block.tensor
        def _(pe):
            pe.wait_ge(consts_loaded, 16 * 9)
            pe.wait_ge(consts_made, 7)
            pe.matmul(total_psum[:, 0, 0:DIM], minus_ln2[:, :], w_f2[:, :], start=True, stop=True)
            pe.matmul(total_psum[:, 0, DIM:2 * DIM], minus_ln2[:, :], w_o2[:, :], start=True, stop=True
                      ).then_inc(bias_mm, 1)

            def node_features(c, tiles):
                b = c[1] % 2
                pe.wait_ge(x_t_loaded[b], landed(c))
                previous(pe, h_left, c, after)
                x3 = x_t[:, b, 0:tiles * P].rearrange("d (p k) -> d k p", k=tiles)
                for k in range(tiles):
                    last = pe.matmul(pre_psum[:, b, k * DIM:(k + 1) * DIM], x3[:, k, :], w_in[:, :],
                                     start=True, stop=True)
                last.then_inc(h_mm, 1)

            run_chunks(pe, node_features, LAST_H)
            pe.wait_ge(bias_made, 6)
            pe.wait_ge(h_left, FULL_CHUNKS + 1)
            pe.wait_ge(flag_made, 1)
            is_narrow = pe.value_load(narrow[0:1, 0:1], min_val=0, max_val=1)

            def first_layer(g):
                b = g[1] % 2
                pe.wait_ge(f_loaded[b], landed(g))
                previous(pe, hidden_done, g, after)
                pe.matmul(pre_psum[:, b, :], w_f1[:, :], f_t[:, b, :], start=True, stop=True).then_inc(pre_done, 1)

            def second_layer(g):
                b = g[1] % 2
                pe.wait_ge(hidden_done, after(g))
                previous(pe, message_done, g, after)
                pe.matmul(filter_psum[:, b, :], ones_bias[:, :], bias_f[:, :, :].rearrange("q k d -> q (k d)"),
                          start=True, stop=False)
                for k in range(TILES):
                    d = slice(k * DIM, (k + 1) * DIM)
                    last = pe.matmul(filter_psum[:, b, d], hidden[:, b, k * P:(k + 1) * P], w_f2[:, :],
                                     start=False, stop=(k == TILES - 1))
                last.then_inc(filter_done, 1)

            def sum_repeated(g):
                b = g[1] % 2
                pe.wait_ge(message_done, after(g))
                pe.wait_ge(same_done, after(g))
                previous(pe, total_done, g, after)
                for k in range(TILES):
                    d = slice(k * DIM, (k + 1) * DIM)
                    last = pe.matmul(total_psum[:, b, d], same[:, b, k * P:(k + 1) * P], message[:, b, d],
                                     start=True, stop=True)
                last.then_inc(total_mm_done, 1)

            def gather(g):
                b = g[1] % 2
                pe.wait_ge(pick_done, after(g))
                pe.wait_ge(window_loaded[b], landed(g))
                previous(pe, h_dst_done, g, after)
                for k in range(TILES):
                    for part in range(3):
                        last = pe.matmul(gather_psum[:, b, k * DIM:(k + 1) * DIM], pick[:, b, k * P:(k + 1) * P],
                                         window[:, b, part, :], start=(part == 0), stop=(part == 2))
                last.then_inc(gather_done, 1)

            def step(i, narrow_form):
                if exists(plus(i, 2)):
                    first_layer(plus(i, 2))
                if exists(i):
                    second_layer(i)
                if exists(plus(i, -1)):
                    sum_repeated(plus(i, -1))
                if narrow_form and exists(plus(i, 1)):
                    gather(plus(i, 1))

            with pe.If(is_narrow):
                run_groups(pe, lambda i: step(i, True), -2)
            with pe.Else():
                run_groups(pe, lambda i: step(i, False), -2)

            pe.wait_ge(total_done, GROUPS)
            pe.wait_ge(message_done, GROUPS)

            def last_layers(i):
                c = plus(i, 1)
                if exists(c, CHUNKS):
                    b, tiles = c[1] % 2, tiles_of(c)
                    pe.wait_ge(e_halves, 2 * after(c))
                    previous(pe, e_agg_sb, c, after)
                    for k in range(tiles):
                        d = slice(k * DIM, (k + 1) * DIM)
                        for s in range(2):
                            last = pe.matmul(filter_psum[:, b, d], half_sum[:, b, s, d], ident[:, :],
                                             start=(s == 0), stop=(s == 1))
                    last.then_inc(e_agg_t, 1)
                c = i
                if exists(c, CHUNKS):
                    b, n = c[1] % 2, tiles_of(c) * P
                    pe.wait_ge(e_agg_sb, after(c))
                    previous(pe, e_hidden, c, after)
                    pe.matmul(pre_psum[:, b, 0:n], w_o1[:, :], agg_t[:, b, 0:n], start=True, stop=True
                              ).then_inc(e_pre, 1)
                c = plus(i, -1)
                if exists(c, CHUNKS):
                    b, tiles = c[1] % 2, tiles_of(c)
                    n = tiles * P
                    pe.wait_ge(e_hidden, after(c))
                    previous(pe, e_row, c, after)
                    pe.matmul(total_psum[:, b, 0:n], ones_bias[:, :],
                              bias_o[:, 0:tiles, :].rearrange("q k d -> q (k d)"), start=True, stop=False)
                    for k in range(tiles):
                        d = slice(k * DIM, (k + 1) * DIM)
                        last = pe.matmul(total_psum[:, b, d], hidden[:, b, k * P:(k + 1) * P], w_o2[:, :],
                                         start=False, stop=(k == tiles - 1))
                    last.then_inc(e_out, 1)

            run_last_layers(pe, last_layers)


def kernel(x, src, dst, edge_attr_20, edge_weight, L0_gnn_W_in2f, L0_gnn_W_filt1, L0_gnn_b_filt1, L0_gnn_W_filt2,
           L0_gnn_b_filt2, L0_gnn_W_out1, L0_gnn_b_out1, L0_gnn_W_out2, L0_gnn_b_out2):
    import concourse.bacc as bacc
    from concourse.bass_utils import run_bass_kernel_spmd

    extra = EDGES_PAD - EDGES
    src_p = np.concatenate([np.asarray(src), np.full(extra, PAD_SRC, np.int32)])
    dst_p = np.pad(np.asarray(dst), (0, extra), mode="edge")

    def columns(a):
        return np.ascontiguousarray(a.reshape(SLOTS * TILES, P).T)

    def filled(a, n):
        return np.pad(np.asarray(a), ((0, n - a.shape[0]), (0, 0)))

    arrays = {
        "x": filled(x, NODE_ROWS),
        "x_t": np.ascontiguousarray(filled(x, WINDOW_ROWS).T),
        "f_t": np.ascontiguousarray(filled(edge_attr_20, EDGES_PAD).T),
        "src": src_p,
        "dst": dst_p,
        "src_cols": columns(src_p),
        "dst_cols": columns(dst_p),
        "weight_cols": columns(np.pad(np.asarray(edge_weight), (0, extra))),
        "w_in": L0_gnn_W_in2f, "w_f1": L0_gnn_W_filt1, "b_f1": L0_gnn_b_filt1,
        "w_f2": L0_gnn_W_filt2, "b_f2": L0_gnn_b_filt2, "w_o1": L0_gnn_W_out1,
        "b_o1": L0_gnn_b_out1, "w_o2": L0_gnn_W_out2, "b_o2": L0_gnn_b_out2,
    }
    arrays = {f"in_{n}": np.ascontiguousarray(a) for n, a in arrays.items()}
    nc = bacc.Bacc("TRN2", target_bir_lowering=False, num_devices=1)
    t = {n[3:]: nc.dram_tensor(n, a.shape, mybir.dt.from_np(a.dtype), kind="ExternalInput").ap()
         for n, a in arrays.items()}
    t["out"] = nc.dram_tensor("out", (NODES, DIM), F32, kind="ExternalOutput").ap()
    build(nc, t)
    return run_bass_kernel_spmd(nc, [arrays], core_ids=[0]).results[0]["out"]
```
